# Optimizing a Trainium2 kernel written in Bass

```python
import numpy as np
import jax
import jax.numpy as jnp

def _softmax(x, axis=-1):
    return jax.nn.softmax(x, axis=axis)

def _gelu(x):
    return jax.nn.gelu(x, approximate=True)

def _silu(x):
    return jax.nn.silu(x)

def _sigmoid(x):
    return jax.nn.sigmoid(x)

def _layernorm(x, axis=-1, eps=1e-05):
    m = jnp.mean(x, axis=axis, keepdims=True)
    v = jnp.var(x, axis=axis, keepdims=True)
    return (x - m) / jnp.sqrt(v + eps)

def _scatter_add(tgt, idx, src, axis=0):
    return tgt.at[idx].add(src)

def _segment_sum(src, seg, n):
    return jax.ops.segment_sum(src, seg, n)
kernel_name = 'mk_dlrm_tower_d1_rec_r8_a3cba7'

def setup_inputs(seed: int=0):
    np.random.seed(seed)
    _w = jnp.asarray

    def _rec_inputs():
        import jax
        import jax.numpy as jnp
        _tk = jax.random.key(seed)
        dense_ctx = jax.random.normal(jax.random.fold_in(_tk, 190), (2048, 16), jnp.float32)
        ids = jnp.stack([jax.random.randint(jax.random.fold_in(_tk, 200 + f), (2048,), 0, v, jnp.int32) for f, v in enumerate([1000, 12500, 125000, 1250, 12500, 1250, 1250, 1000, 1000, 1250, 12500, 1250, 125000, 1000, 125000, 1000, 1250, 1250, 1000, 1000, 1000, 1250, 1250, 12500, 1000, 1250, 1000, 1000, 12500, 12500, 1000, 1250])], axis=1)
        tbl_0 = 0.05 * jax.random.normal(jax.random.fold_in(_tk, 500 + 0), (1000, 64), jnp.float32)
        tbl_1 = 0.05 * jax.random.normal(jax.random.fold_in(_tk, 500 + 1), (12500, 64), jnp.float32)
        tbl_2 = 0.05 * jax.random.normal(jax.random.fold_in(_tk, 500 + 2), (125000, 64), jnp.float32)
        tbl_3 = 0.05 * jax.random.normal(jax.random.fold_in(_tk, 500 + 3), (1250, 64), jnp.float32)
        tbl_4 = 0.05 * jax.random.normal(jax.random.fold_in(_tk, 500 + 4), (12500, 64), jnp.float32)
        tbl_5 = 0.05 * jax.random.normal(jax.random.fold_in(_tk, 500 + 5), (1250, 64), jnp.float32)
        tbl_6 = 0.05 * jax.random.normal(jax.random.fold_in(_tk, 500 + 6), (1250, 64), jnp.float32)
        tbl_7 = 0.05 * jax.random.normal(jax.random.fold_in(_tk, 500 + 7), (1000, 64), jnp.float32)
        tbl_8 = 0.05 * jax.random.normal(jax.random.fold_in(_tk, 500 + 8), (1000, 64), jnp.float32)
        tbl_9 = 0.05 * jax.random.normal(jax.random.fold_in(_tk, 500 + 9), (1250, 64), jnp.float32)
        tbl_10 = 0.05 * jax.random.normal(jax.random.fold_in(_tk, 500 + 10), (12500, 64), jnp.float32)
        tbl_11 = 0.05 * jax.random.normal(jax.random.fold_in(_tk, 500 + 11), (1250, 64), jnp.float32)
        tbl_12 = 0.05 * jax.random.normal(jax.random.fold_in(_tk, 500 + 12), (125000, 64), jnp.float32)
        tbl_13 = 0.05 * jax.random.normal(jax.random.fold_in(_tk, 500 + 13), (1000, 64), jnp.float32)
        tbl_14 = 0.05 * jax.random.normal(jax.random.fold_in(_tk, 500 + 14), (125000, 64), jnp.float32)
        tbl_15 = 0.05 * jax.random.normal(jax.random.fold_in(_tk, 500 + 15), (1000, 64), jnp.float32)
        tbl_16 = 0.05 * jax.random.normal(jax.random.fold_in(_tk, 500 + 16), (1250, 64), jnp.float32)
        tbl_17 = 0.05 * jax.random.normal(jax.random.fold_in(_tk, 500 + 17), (1250, 64), jnp.float32)
        tbl_18 = 0.05 * jax.random.normal(jax.random.fold_in(_tk, 500 + 18), (1000, 64), jnp.float32)
        tbl_19 = 0.05 * jax.random.normal(jax.random.fold_in(_tk, 500 + 19), (1000, 64), jnp.float32)
        tbl_20 = 0.05 * jax.random.normal(jax.random.fold_in(_tk, 500 + 20), (1000, 64), jnp.float32)
        tbl_21 = 0.05 * jax.random.normal(jax.random.fold_in(_tk, 500 + 21), (1250, 64), jnp.float32)
        tbl_22 = 0.05 * jax.random.normal(jax.random.fold_in(_tk, 500 + 22), (1250, 64), jnp.float32)
        tbl_23 = 0.05 * jax.random.normal(jax.random.fold_in(_tk, 500 + 23), (12500, 64), jnp.float32)
        tbl_24 = 0.05 * jax.random.normal(jax.random.fold_in(_tk, 500 + 24), (1000, 64), jnp.float32)
        tbl_25 = 0.05 * jax.random.normal(jax.random.fold_in(_tk, 500 + 25), (1250, 64), jnp.float32)
        tbl_26 = 0.05 * jax.random.normal(jax.random.fold_in(_tk, 500 + 26), (1000, 64), jnp.float32)
        tbl_27 = 0.05 * jax.random.normal(jax.random.fold_in(_tk, 500 + 27), (1000, 64), jnp.float32)
        tbl_28 = 0.05 * jax.random.normal(jax.random.fold_in(_tk, 500 + 28), (12500, 64), jnp.float32)
        tbl_29 = 0.05 * jax.random.normal(jax.random.fold_in(_tk, 500 + 29), (12500, 64), jnp.float32)
        tbl_30 = 0.05 * jax.random.normal(jax.random.fold_in(_tk, 500 + 30), (1000, 64), jnp.float32)
        tbl_31 = 0.05 * jax.random.normal(jax.random.fold_in(_tk, 500 + 31), (1250, 64), jnp.float32)
        _rk = jax.random.fold_in(_tk, 7)
        W_top1 = 0.0441942 * jax.random.normal(jax.random.fold_in(_tk, 801), (512, 512), jnp.float32)
        W_top2 = 0.0441942 * jax.random.normal(jax.random.fold_in(_tk, 802), (512, 256), jnp.float32)
        W_top3 = 0.0625 * jax.random.normal(jax.random.fold_in(_tk, 803), (256, 1), jnp.float32)
        b_top1 = jnp.zeros((512,), jnp.float32)
        b_top2 = jnp.zeros((256,), jnp.float32)
        return (dense_ctx, ids, tbl_0, tbl_1, tbl_2, tbl_3, tbl_4, tbl_5, tbl_6, tbl_7, tbl_8, tbl_9, tbl_10, tbl_11, tbl_12, tbl_13, tbl_14, tbl_15, tbl_16, tbl_17, tbl_18, tbl_19, tbl_20, tbl_21, tbl_22, tbl_23, tbl_24, tbl_25, tbl_26, tbl_27, tbl_28, tbl_29, tbl_30, tbl_31, W_top1, b_top1, W_top2, b_top2, W_top3)
    dense_ctx, ids, tbl_0, tbl_1, tbl_2, tbl_3, tbl_4, tbl_5, tbl_6, tbl_7, tbl_8, tbl_9, tbl_10, tbl_11, tbl_12, tbl_13, tbl_14, tbl_15, tbl_16, tbl_17, tbl_18, tbl_19, tbl_20, tbl_21, tbl_22, tbl_23, tbl_24, tbl_25, tbl_26, tbl_27, tbl_28, tbl_29, tbl_30, tbl_31, W_top1, b_top1, W_top2, b_top2, W_top3 = _rec_inputs()

    def _L0_rec_setup():
        import jax, jax.numpy as jnp
        import numpy as np
        NUM_FIELDS = 32
        BATCH = 2048
        EMBED_DIM = 64
        _pairs = np.array([(i, j) for i in range(NUM_FIELDS - 1) for j in range(i + 1, NUM_FIELDS)], dtype=np.int32)
        ROW = jnp.asarray(_pairs[:, 0])
        COL = jnp.asarray(_pairs[:, 1])
        key = jax.random.key(seed)
        x = jax.random.normal(key, (BATCH, NUM_FIELDS, EMBED_DIM), dtype=jnp.float32)
        return {'x': x}
    _L0_rec_all = _L0_rec_setup()
    _L0_rec_in = {k: v for k, v in _L0_rec_all.items() if k in ()}
    del _L0_rec_all
    return {'dense_ctx': dense_ctx, 'ids': ids, 'tbl_0': tbl_0, 'tbl_1': tbl_1, 'tbl_2': tbl_2, 'tbl_3': tbl_3, 'tbl_4': tbl_4, 'tbl_5': tbl_5, 'tbl_6': tbl_6, 'tbl_7': tbl_7, 'tbl_8': tbl_8, 'tbl_9': tbl_9, 'tbl_10': tbl_10, 'tbl_11': tbl_11, 'tbl_12': tbl_12, 'tbl_13': tbl_13, 'tbl_14': tbl_14, 'tbl_15': tbl_15, 'tbl_16': tbl_16, 'tbl_17': tbl_17, 'tbl_18': tbl_18, 'tbl_19': tbl_19, 'tbl_20': tbl_20, 'tbl_21': tbl_21, 'tbl_22': tbl_22, 'tbl_23': tbl_23, 'tbl_24': tbl_24, 'tbl_25': tbl_25, 'tbl_26': tbl_26, 'tbl_27': tbl_27, 'tbl_28': tbl_28, 'tbl_29': tbl_29, 'tbl_30': tbl_30, 'tbl_31': tbl_31, 'W_top1': W_top1, 'b_top1': b_top1, 'W_top2': W_top2, 'b_top2': b_top2, 'W_top3': W_top3}

def reference(dense_ctx, ids, tbl_0, tbl_1, tbl_2, tbl_3, tbl_4, tbl_5, tbl_6, tbl_7, tbl_8, tbl_9, tbl_10, tbl_11, tbl_12, tbl_13, tbl_14, tbl_15, tbl_16, tbl_17, tbl_18, tbl_19, tbl_20, tbl_21, tbl_22, tbl_23, tbl_24, tbl_25, tbl_26, tbl_27, tbl_28, tbl_29, tbl_30, tbl_31, W_top1, b_top1, W_top2, b_top2, W_top3):
    import jax
    import jax.numpy as jnp

    def _L0_rec_ref(x):
        import jax, jax.numpy as jnp
        import numpy as np
        NUM_FIELDS = 32
        BATCH = 2048
        EMBED_DIM = 64
        _pairs = np.array([(i, j) for i in range(NUM_FIELDS - 1) for j in range(i + 1, NUM_FIELDS)], dtype=np.int32)
        ROW = jnp.asarray(_pairs[:, 0])
        COL = jnp.asarray(_pairs[:, 1])
        s = jnp.sum(x, axis=-1)
        return s[:, ROW] * s[:, COL]
    e = jnp.stack([tbl_0[ids[:, 0]], tbl_1[ids[:, 1]], tbl_2[ids[:, 2]], tbl_3[ids[:, 3]], tbl_4[ids[:, 4]], tbl_5[ids[:, 5]], tbl_6[ids[:, 6]], tbl_7[ids[:, 7]], tbl_8[ids[:, 8]], tbl_9[ids[:, 9]], tbl_10[ids[:, 10]], tbl_11[ids[:, 11]], tbl_12[ids[:, 12]], tbl_13[ids[:, 13]], tbl_14[ids[:, 14]], tbl_15[ids[:, 15]], tbl_16[ids[:, 16]], tbl_17[ids[:, 17]], tbl_18[ids[:, 18]], tbl_19[ids[:, 19]], tbl_20[ids[:, 20]], tbl_21[ids[:, 21]], tbl_22[ids[:, 22]], tbl_23[ids[:, 23]], tbl_24[ids[:, 24]], tbl_25[ids[:, 25]], tbl_26[ids[:, 26]], tbl_27[ids[:, 27]], tbl_28[ids[:, 28]], tbl_29[ids[:, 29]], tbl_30[ids[:, 30]], tbl_31[ids[:, 31]]], axis=1)
    z = _L0_rec_ref(e)
    z = z.reshape(z.shape[0], -1)
    h = jnp.concatenate([z, dense_ctx], axis=1)
    h = jnp.maximum(h @ W_top1 + b_top1, 0.0)
    h = jnp.maximum(h @ W_top2 + b_top2, 0.0)
    y = h @ W_top3
    return y

_drawn_inputs = setup_inputs


def setup_inputs(seed=0):
    import zlib

    import numpy as np

    out = dict(_drawn_inputs(seed))
    spreads = {'b_top1': (0.0, 0.1), 'b_top2': (0.0, 0.1)}
    factors = {}
    for name, (base, spread) in spreads.items():
        noise = np.random.default_rng([zlib.crc32(name.encode()), seed]).standard_normal(out[name].shape)
        drawn = base * np.exp(spread * noise) if base else spread * noise
        out[name] = jnp.asarray(drawn.astype(out[name].dtype))
    for name, factor in factors.items():
        out[name] = (out[name] * factor).astype(out[name].dtype)
    return out
```

```python
from contextlib import ExitStack

import concourse.bass as bass
import numpy as np
from concourse import mybir

P = 128
BATCH, FIELDS, DIM = 2048, 32, 64
VOCAB = [1000, 12500, 125000, 1250, 12500, 1250, 1250, 1000, 1000, 1250, 12500, 1250, 125000, 1000, 125000, 1000,
         1250, 1250, 1000, 1000, 1000, 1250, 1250, 12500, 1000, 1250, 1000, 1000, 12500, 12500, 1000, 1250]
GATHERED = [f for v in (125000, 12500) for f in range(FIELDS) if VOCAB[f] == v]
SMALL = [f for v in (1250, 1000) for f in range(FIELDS) if VOCAB[f] == v]
NG, NS = len(GATHERED), len(SMALL)
DENSE = 16
PAIRS = [(i, j) for i in range(FIELDS - 1) for j in range(i + 1, FIELDS)]
H1, H2 = 512, 256

CHUNKS = BATCH // P
TILE_CHUNKS = 2
TB = TILE_CHUNKS * P
TILES = BATCH // TB
TURNS = TILES // 2

ROWS_PER_PARTITION = 10
R = ROWS_PER_PARTITION
PARTS = 3
STRIPS = 4
STRIP = P // STRIPS
PACKS = (NS + STRIPS - 1) // STRIPS
SLOTS = STRIPS * PACKS
PAIRS_OF_PACKS = PACKS // 2
PLACE = {f: n for n, f in enumerate(GATHERED + SMALL)}
SUMROWS = PARTS * FIELDS

KT = H1 // P
NT2 = H2 // P
PAIR_ROWS_LAST = len(PAIRS) - (KT - 1) * P

GATHERS = NG * TILE_CHUNKS
GROUPS = 3
PER_GROUP = GATHERS // GROUPS
BROADCASTS = 1 + STRIPS

ROUND = 12582912.0


BF16_ONE = np.uint16(0x3F80)


def table_pieces(vocab):
    partitions = vocab // R
    main = partitions // 16 * 16
    return [(0, main), (main, partitions - main)]


def constants():
    gather_rows = np.zeros((P, PACKS, SUMROWS))
    for s in range(NS):
        g, q = divmod(s, PACKS)
        for part in range(PARTS):
            for r in range(R):
                gather_rows[g * STRIP + part * R + r, q, part * FIELDS + NG + s] = 1
    pair = np.zeros((P, KT, 2, P))
    for n, ij in enumerate(PAIRS):
        for side in range(2):
            for part in range(PARTS):
                pair[part * FIELDS + PLACE[ij[side]], n // P, side, n % P] = 1
    ones = np.concatenate([gather_rows.reshape(P, -1), pair.reshape(P, -1), np.eye(P)], axis=1)
    counters = np.zeros((P, 2), np.float32)
    counters[:, 0] = np.arange(P)
    x = np.arange(P) % STRIP
    counters[:, 1] = np.where(x < PARTS * R, x % R, -1)
    return ones.astype(np.uint16) * BF16_ONE, counters


def dlrm_tower(nc, ids_rows, ids_slots, dense_t, tables, W1, b1, W2, b2, W3, ones, counters, out):
    fp32, bf16, i32 = mybir.dt.float32, mybir.dt.bfloat16, mybir.dt.int32
    ALU, ACT, AX = mybir.AluOpType, mybir.ActivationFunctionType, mybir.AxisListType

    ctx = ExitStack()
    with ctx:
        def sb(name, shape, dt):
            return ctx.enter_context(nc.sbuf_tensor(name, shape, dt))

        def pb(name):
            return ctx.enter_context(nc.psum_tensor(name, [P, 512], fp32))

        def sem(name):
            return ctx.enter_context(nc.semaphore(name))

        ones_sb = sb("ones_sb", list(ones.shape), bf16)
        sel_rows = ones_sb[:, 0:PACKS * SUMROWS].rearrange("p (q m) -> p q m", q=PACKS)
        sel_pair = ones_sb[0:SUMROWS, PACKS * SUMROWS:PACKS * SUMROWS + KT * 2 * P].rearrange(
            "p (k s m) -> p k s m", k=KT, s=2)
        ident = ones_sb[:, PACKS * SUMROWS + KT * 2 * P:]
        count_sb = sb("count_sb", [P, 2], fp32)
        block_of_p, row_of_p = count_sb[:, 0:1], count_sb[:, 1:2]
        W1_sb = sb("W1_sb", [P, KT, H1], fp32)
        W2_sb = sb("W2_sb", [P, KT, H2], fp32)
        W3_sb = sb("W3_sb", [P, NT2], fp32)
        b1_sb = sb("b1_sb", [P, KT], fp32)
        b2_sb = sb("b2_sb", [P, NT2], fp32)
        rows = sb("rows", [P, NS, R * DIM], fp32)
        sums = sb("sums", [P, SLOTS, R], fp32)
        rest = sb("rest", [P, 2, SLOTS, R], fp32)
        sum_parts = sb("sum_parts", [P, SLOTS, STRIP], bf16)
        number = sb("number", [P, SLOTS * BATCH // P], i32)
        scaled = sb("scaled", [P, SLOTS * BATCH // P], fp32)
        block = sb("block", [P, SLOTS * BATCH // P], fp32)
        block_bf = sb("block_bf", [P, SLOTS * BATCH // P], bf16)
        row_bf = sb("row_bf", [P, SLOTS * BATCH // P], bf16)
        blocks_dram = nc.dram_tensor("blocks_dram", [TILES, SLOTS * TB], bf16).ap()
        row_dram = nc.dram_tensor("row_dram", [TILES, SLOTS * TB], bf16).ap()
        block_all = sb("block_all", [P, 2, SLOTS * TB], bf16)
        row_all = sb("row_all", [P, 2, PACKS, TB], bf16)
        onehot = sb("onehot", [P, 2, SLOTS, TB], bf16)
        picked = sb("picked", [P, 2, PACKS, TB], bf16)
        index = sb("index", [P, 2, TILE_CHUNKS, FIELDS], i32)
        gathered = sb("gathered", [P, 2, GATHERS, DIM], fp32)
        gsum = sb("gsum", [P, 2, NG, TILE_CHUNKS], fp32)
        grest = sb("grest", [P, 2, 2, NG, TILE_CHUNKS], fp32)
        gparts = sb("gparts", [P, 2, TILE_CHUNKS, PARTS, FIELDS], bf16)
        sums_t = sb("sums_t", [SUMROWS, 2, TB], bf16)
        right = sb("right", [P, 2, 2, TB], fp32)
        z = sb("z", [P, 2, KT, TB], fp32)
        h1 = sb("h1", [P, KT, TB], fp32)
        h2 = sb("h2", [P, NT2, TB], fp32)
        y_all = sb("y_all", [P, CHUNKS], fp32)

        ps_look = [pb("ps_look0"), pb("ps_look1")]
        ps_s = pb("ps_s")
        ps_left, ps_right = pb("ps_left"), pb("ps_right")
        ps_h1 = [pb("ps_h1a"), pb("ps_h1b")]
        ps_h2 = pb("ps_h2")
        ps_sum = ps_s[0:SUMROWS, 0:TB]
        ps_l, ps_r = [ps_left, ps_h1[0]], [ps_right, ps_h1[1]]
        ps_second = [ps_h2[:, 0:TB], ps_h1[0][:, 0:TB]]
        ps_y = ps_h1[1][:, 0:TILE_CHUNKS]

        ids_in = sem("ids_in")
        const_in = sem("const_in")
        count_in = sem("count_in")
        weights_in = sem("weights_in")
        bias_in = sem("bias_in")
        table_in = [sem(f"table_in{q}") for q in range(PACKS)]
        blocks_found = sem("blocks_found")
        blocks_stored = sem("blocks_stored")
        broadcast_in = [sem(f"broadcast_in{b}") for b in range(2)]
        index_in = [sem(f"index_in{b}") for b in range(2)]
        dense_in = [sem(f"dense_in{b}") for b in range(2)]
        gather_in = [[sem(f"gather_in{b}{g}") for g in range(GROUPS)] for b in range(2)]
        dve_step = sem("dve_step")
        tables_split = sem("tables_split")
        onehot_built = sem("onehot_built")
        looked_up = sem("looked_up")
        row_picked = sem("row_picked")
        gather_summed = sem("gather_summed")
        gather_split = sem("gather_split")
        sums_in_psum = sem("sums_in_psum")
        sums_copied = sem("sums_copied")
        pairs_in_psum = sem("pairs_in_psum")
        right_copied = sem("right_copied")
        z_ready = sem("z_ready")
        h1_in_psum = sem("h1_in_psum")
        h1_ready = sem("h1_ready")
        h2_in_psum = sem("h2_in_psum")
        h2_ready = sem("h2_ready")
        y_in_psum = sem("y_in_psum")
        y_free = sem("y_free")
        out_written = sem("out_written")

        def load_tables(eng, pieces):
            for s, first, n in pieces:
                eng.dma_start(rows[first:first + n, s, :],
                              tables[SMALL[s]][first * R:(first + n) * R, :].rearrange("(p r) d -> p (r d)", r=R)
                              ).then_inc(table_in[s % PACKS], 16)

        def pieces_of_pack(q):
            return [(g * PACKS + q, *piece) for g in range(STRIPS) if g * PACKS + q < NS
                    for piece in table_pieces(VOCAB[SMALL[g * PACKS + q]])]

        table_pieces_in_order = [x for q in range(PACKS) for x in pieces_of_pack(q)]

        bl = ctx.enter_context(nc.Block())

        @bl.sync
        def _(sp):
            def load_tile(t, b):
                sp.dma_start(block_all[:, b, :],
                             blocks_dram[bass.ds(t, 1), :].broadcast_to([P, SLOTS * TB])
                             ).then_inc(broadcast_in[b], 16)

            def load_rows(t, b):
                for g in range(STRIPS):
                    sp.dma_start(row_all[g * STRIP:(g + 1) * STRIP, b, :, :].rearrange("p q n -> p (q n)"),
                                 row_dram[bass.ds(t, 1), g * PACKS * TB:(g + 1) * PACKS * TB]
                                 .broadcast_to([STRIP, PACKS * TB])).then_inc(broadcast_in[b], 16)

            def load_index(t, b):
                sp.dma_start(index[:, b, :, :], ids_rows[:, bass.ds(t * TILE_CHUNKS, TILE_CHUNKS), :]
                             ).then_inc(index_in[b], 16)

            def load_dense(t, b):
                sp.dma_start(z[PAIR_ROWS_LAST:P, b, KT - 1, :], dense_t[:, bass.ds(t * TB, TB)]
                             ).then_inc(dense_in[b], 16)

            sp.dma_start(number[:, :], ids_slots).then_inc(ids_in, 16)
            for t in range(2):
                load_index(t, t)
            sp.dma_start(count_sb[:, :], counters).then_inc(count_in, 16)
            load_tables(sp, table_pieces_in_order[0:14:2])
            sp.wait_ge(blocks_found, 2)
            sp.dma_start(blocks_dram.rearrange("t n -> (t n)").rearrange("(p x) -> p x", p=P), block_bf[:, :]
                         ).then_inc(blocks_stored, 16)
            sp.dma_start(row_dram.rearrange("t n -> (t n)").rearrange("(p x) -> p x", p=P), row_bf[:, :]
                         ).then_inc(blocks_stored, 16)
            load_tables(sp, table_pieces_in_order[14:20:2])
            sp.wait_ge(blocks_stored, 32)
            for t in range(2):
                load_tile(t, t)
                load_rows(t, t)
            load_tables(sp, table_pieces_in_order[20::2])
            for t in range(2):
                load_dense(t, t)
            with sp.Fori(0, TURNS - 1) as turn:
                for b in range(2):
                    t = turn * 2 + b
                    sp.wait_ge(onehot_built, t + 1)
                    load_tile(t + 2, b)
                    sp.wait_ge(row_picked, t * PAIRS_OF_PACKS + PAIRS_OF_PACKS)
                    load_rows(t + 2, b)
                    sp.wait_ge(gather_summed, t * GROUPS + GROUPS)
                    load_index(t + 2, b)
                    sp.wait_ge(h1_in_psum, t * 2 + 2)
                    load_dense(t + 2, b)
            sp.wait_ge(y_free, TILES + 1)
            sp.dma_start(out, y_all[:, :]).then_inc(out_written, 16)
            sp.wait_ge(out_written, 16)

        @bl.gpsimd
        def _(pool):
            for t in range(TILES):
                b = t % 2
                pool.wait_ge(index_in[b], 16 * (t // 2 + 1))
                for n in range(GATHERS):
                    f, c = divmod(n, TILE_CHUNKS)
                    if t >= 2 and n % PER_GROUP == 0:
                        pool.wait_ge(gather_summed, (t - 2) * GROUPS + n // PER_GROUP + 1)
                    pool.indirect_dma_start(
                        gathered[:, b, n, :], None, tables[GATHERED[f]],
                        bass.IndirectOffsetOnAxis(index[:, b, c, GATHERED[f]:GATHERED[f] + 1], 0)
                    ).then_inc(gather_in[b][n // PER_GROUP], 16)

        @bl.scalar
        def _(act):
            act.dma_start(ones_sb[:, :], ones.bitcast(bf16)).then_inc(const_in, 16)
            load_tables(act, table_pieces_in_order[1::2])
            act.dma_start(b1_sb[:, :], b1).then_inc(bias_in, 16)
            act.dma_start(b2_sb[:, :], b2).then_inc(bias_in, 16)
            act.dma_start(W1_sb[:, :, :], W1.rearrange("(k p) n -> p k n", p=P)).then_inc(weights_in, 16)
            act.dma_start(W2_sb[:, :, :], W2.rearrange("(k p) n -> p k n", p=P)).then_inc(weights_in, 16)
            act.dma_start(W3_sb[:, :], W3).then_inc(weights_in, 16)

            act.wait_ge(bias_in, 32)
            act.nop().then_inc(y_free, 1)

            def tile(t, b):
                act.wait_ge(sums_in_psum, t + 1)
                act.activation(sums_t[:, b, :], ps_sum, ACT.Copy).then_inc(sums_copied, 1)
                for half in range(2):
                    act.wait_ge(pairs_in_psum, t * 2 + half + 1)
                    act.activation(right[:, half, :, :].rearrange("p k n -> p (k n)"), ps_r[half][:, :], ACT.Copy
                                   ).then_inc(right_copied, 1)
                for k in range(KT):
                    if k % 2 == 0:
                        act.wait_ge(h1_in_psum, t * 2 + k // 2 + 1)
                    act.activation(h1[:, k, :], ps_h1[k // 2][:, k % 2 * TB:(k % 2 + 1) * TB], ACT.Relu,
                                   bias=b1_sb[:, k:k + 1]).then_inc(h1_ready, 1)
                for k in range(NT2):
                    act.wait_ge(h2_in_psum, t * NT2 + k + 1)
                    act.activation(h2[:, k, :], ps_second[k], ACT.Relu,
                                   bias=b2_sb[:, k:k + 1]).then_inc(h2_ready, 1)
                act.wait_ge(y_in_psum, t + 1)
                act.activation(y_all[:, bass.ds(t * TILE_CHUNKS, TILE_CHUNKS)], ps_y, ACT.Copy
                               ).then_inc(y_free, 1)

            with act.Fori(0, TURNS) as turn:
                for b in range(2):
                    tile(turn * 2 + b, b)

        @bl.vector
        def _(dve):
            steps = [0]

            def step(instruction, base=0):
                steps[0] += 1
                instruction.then_inc(dve_step, 1)
                dve.wait_ge(dve_step, base + steps[0])

            def split(parts, value, left, base=0):
                step(dve.tensor_copy(parts[0], value), base)
                step(dve.tensor_tensor(left[0], value, parts[0], ALU.subtract), base)
                step(dve.tensor_copy(parts[1], left[0]), base)
                step(dve.tensor_tensor(left[1], left[0], parts[1], ALU.subtract), base)
                return dve.tensor_copy(parts[2], left[1])

            def build_onehot(t, b, arrivals):
                dve.wait_ge(broadcast_in[b], arrivals)
                dve.tensor_scalar(onehot[:, b, :, :].rearrange("p s n -> p (s n)"), block_all[:, b, :],
                                  block_of_p, None, ALU.is_equal).then_inc(onehot_built, 1)

            def pick_rows(t, b):
                for i in range(PAIRS_OF_PACKS):
                    dve.wait_ge(looked_up, t * PAIRS_OF_PACKS + i + 1)
                    dve.scalar_tensor_tensor(
                        picked[:, b, 2 * i:2 * i + 2, :].rearrange("p q n -> p (q n)"),
                        row_all[:, b, 2 * i:2 * i + 2, :].rearrange("p q n -> p (q n)"),
                        row_of_p, ps_look[i % 2][:, :], ALU.is_equal, ALU.mult).then_inc(row_picked, 1)

            def tile(t, b, base):
                for g in range(GROUPS):
                    dve.wait_ge(gather_in[b][g], (t + 2 - b) * 8 * PER_GROUP)
                    n = slice(g * PER_GROUP, (g + 1) * PER_GROUP)
                    last = dve.tensor_reduce(gsum[:, b, :, :].rearrange("p f c -> p (f c)")[:, n],
                                             gathered[:, b, n, :], AX.X, ALU.add).then_inc(gather_summed, 1)
                dve.wait_ge(gather_summed, t * GROUPS + GROUPS)
                split([gparts[:, b, :, k, 0:NG].rearrange("p c f -> p f c") for k in range(PARTS)],
                      gsum[:, b, :, :], [grest[:, b, k, :, :] for k in range(2)], base).then_inc(gather_split, 1)
                for half in range(2):
                    dve.wait_ge(right_copied, t * 2 + half + 1)
                    if half == 0:
                        dve.tensor_tensor(z[:, b, 0:2, :].rearrange("p k n -> p (k n)"), ps_l[0][:, :],
                                          right[:, 0, :, :].rearrange("p k n -> p (k n)"), ALU.mult
                                          ).then_inc(z_ready, 1)
                    else:
                        dve.tensor_tensor(z[:, b, 2, :], ps_l[1][:, 0:TB], right[:, 1, 0, :], ALU.mult
                                          ).then_inc(z_ready, 1)
                        dve.tensor_tensor(z[0:PAIR_ROWS_LAST, b, 3, :], ps_l[1][0:PAIR_ROWS_LAST, TB:2 * TB],
                                          right[0:PAIR_ROWS_LAST, 1, 1, :], ALU.mult).then_inc(z_ready, 1)

            dve.wait_ge(ids_in, 16)
            step(dve.tensor_scalar(scaled[:, :], number[:, :], 1.0 / R, -0.45, ALU.mult, ALU.add))
            step(dve.tensor_scalar(block[:, :], scaled[:, :], ROUND, -ROUND, ALU.add, ALU.add))
            dve.tensor_copy(block_bf[:, :], block[:, :]).then_inc(blocks_found, 1)
            dve.scalar_tensor_tensor(row_bf[:, :], block[:, :], -float(R), number[:, :], ALU.mult, ALU.add
                                     ).then_inc(blocks_found, 1)
            dve.memset(sums[:, :, :], 0.0).then_inc(dve_step, 1)
            dve.memset(sum_parts[:, :, :], 0.0).then_inc(dve_step, 1)
            dve.memset(gparts[:, :, :, :, :], 0.0).then_inc(dve_step, 1)
            steps[0] += 3
            dve.wait_ge(dve_step, steps[0])
            dve.wait_ge(count_in, 16)
            for i in range(PAIRS_OF_PACKS):
                for q in (2 * i, 2 * i + 1):
                    dve.wait_ge(table_in[q], 16 * len(pieces_of_pack(q)))
                    for s in range(q, NS, PACKS):
                        n = VOCAB[SMALL[s]] // R
                        dve.tensor_reduce(sums[0:n, s, :], rows[0:n, s, :].rearrange("p (r d) -> p r d", d=DIM),
                                          AX.X, ALU.add).then_inc(dve_step, 1)
                        steps[0] += 1
                dve.wait_ge(dve_step, steps[0])

                def of_pair(x):
                    return x.rearrange("p (g q) r -> p g q r", g=STRIPS)[:, :, 2 * i:2 * i + 2, :]

                split([of_pair(sum_parts[:, :, k * R:(k + 1) * R]) for k in range(PARTS)],
                      of_pair(sums[:, :, :]), [of_pair(rest[:, k, :, :]) for k in range(2)]).then_inc(tables_split, 1)
                if i == 0:
                    build_onehot(0, 0, 16 * BROADCASTS)
            pick_rows(0, 0)

            before = steps[0]
            per_tile = 4
            with dve.Fori(0, TURNS - 1) as turn:
                for b in range(2):
                    t = turn * 2 + b
                    steps[0] = before
                    build_onehot(t + 1, 1 - b, (turn + 1 + b) * 16 * BROADCASTS)
                    tile(t, b, t * per_tile)
                    pick_rows(t + 1, 1 - b)
            for b in range(2):
                t = TILES - 2 + b
                steps[0] = before
                if b == 0:
                    build_onehot(t + 1, 1, TURNS * 16 * BROADCASTS)
                tile(t, b, t * per_tile)
                if b == 0:
                    pick_rows(t + 1, 1)

        @bl.tensor
        def _(pe):
            def look_up(t, b, i):
                for q in (2 * i, 2 * i + 1):
                    for g in range(STRIPS):
                        s = g * PACKS + q
                        last = pe.matmul(ps_look[i % 2][g * STRIP:(g + 1) * STRIP, q % 2 * TB:(q % 2 + 1) * TB],
                                         sum_parts[:, s, :], onehot[:, b, s, :], start=True, stop=True,
                                         tile_position=(0, g * STRIP))
                last.then_inc(looked_up, 1)

            def look_up_start(t, b):
                pe.wait_ge(onehot_built, t + 1)
                for i in range(PAIRS_OF_PACKS - 1):
                    look_up(t, b, i)

            def look_up_end(t, b):
                pe.wait_ge(row_picked, t * PAIRS_OF_PACKS + 1)
                look_up(t, b, PAIRS_OF_PACKS - 1)

            def tile(t, b, more):
                pe.wait_ge(row_picked, t * PAIRS_OF_PACKS + PAIRS_OF_PACKS)
                for q in range(PACKS):
                    pe.matmul(ps_sum, sel_rows[:, q, :], picked[:, b, q, :], start=(q == 0), stop=False)
                pe.wait_ge(gather_split, t + 1)
                for c in range(TILE_CHUNKS):
                    last = pe.matmul(ps_sum[:, c * P:(c + 1) * P],
                                     gparts[:, b, c, :, :].rearrange("p k f -> p (k f)"), ident,
                                     start=False, stop=(c == TILE_CHUNKS - 1))
                last.then_inc(sums_in_psum, 1)
                pe.wait_ge(sums_copied, t + 1)
                for half in range(2):
                    if half == 1:
                        pe.wait_ge(y_free, t + 1)
                    for k in range(2):
                        for side, ps in enumerate((ps_l[half], ps_r[half])):
                            last = pe.matmul(ps[:, k * TB:(k + 1) * TB], sel_pair[:, 2 * half + k, side, :],
                                             sums_t[:, b, :], start=True, stop=True)
                    last.then_inc(pairs_in_psum, 1)
                if more:
                    look_up_start(t + 1, 1 - b)
                pe.wait_ge(dense_in[b], (t + 2 - b) * 8)
                pe.wait_ge(z_ready, t * 3 + 3)
                for n in range(KT):
                    for k in range(KT):
                        last = pe.matmul(ps_h1[n // 2][:, n % 2 * TB:(n % 2 + 1) * TB],
                                         W1_sb[:, k, n * P:(n + 1) * P], z[:, b, k, :],
                                         start=(k == 0), stop=(k == KT - 1))
                    if n % 2:
                        last.then_inc(h1_in_psum, 1)
                if more:
                    look_up_end(t + 1, 1 - b)
                for n in range(NT2):
                    for k in range(KT):
                        if n == 0:
                            pe.wait_ge(h1_ready, t * KT + k + 1)
                        last = pe.matmul(ps_second[n], W2_sb[:, k, n * P:(n + 1) * P], h1[:, k, :],
                                         start=(k == 0), stop=(k == KT - 1))
                    last.then_inc(h2_in_psum, 1)
                pe.wait_ge(h2_ready, t * NT2 + NT2)
                for c in range(TILE_CHUNKS):
                    for k in range(NT2):
                        last = pe.matmul(ps_y[:, c:c + 1], h2[:, k, c * P:(c + 1) * P], W3_sb[:, k:k + 1],
                                         start=(k == 0), stop=(k == NT2 - 1))
                last.then_inc(y_in_psum, 1)

            pe.wait_ge(const_in, 16)
            pe.wait_ge(onehot_built, 1)
            for i in range(PAIRS_OF_PACKS):
                pe.wait_ge(tables_split, i + 1)
                if i == PAIRS_OF_PACKS - 1:
                    pe.wait_ge(row_picked, 1)
                look_up(0, 0, i)
            pe.wait_ge(weights_in, 48)
            with pe.Fori(0, TURNS - 1) as turn:
                for b in range(2):
                    tile(turn * 2 + b, b, True)
            for b in range(2):
                tile(TILES - 2 + b, b, b == 0)


def kernel(**inputs):
    import concourse.bacc as _bacc
    from concourse.bass_utils import run_bass_kernel_spmd as _run

    nc = _bacc.Bacc("TRN2", target_bir_lowering=False, num_devices=1)
    a = {k: np.ascontiguousarray(v) for k, v in inputs.items()}
    ids = a["ids"].reshape(P, CHUNKS, FIELDS)
    by_slot = ids[:, :, SMALL + [SMALL[-1]] * (SLOTS - NS)].reshape(P, TILES, TILE_CHUNKS, SLOTS)
    ones, counters = constants()
    arrays = {
        "ids_rows": ids,
        "ids_slots": by_slot.transpose(1, 3, 2, 0).reshape(P, SLOTS * BATCH // P),
        "dense_t": a["dense_ctx"].reshape(P, CHUNKS, DENSE).transpose(2, 1, 0).reshape(DENSE, BATCH),
        "W1": a["W_top1"], "b1": a["b_top1"].reshape(KT, P).T,
        "W2": a["W_top2"], "b2": a["b_top2"].reshape(NT2, P).T,
        "W3": a["W_top3"].reshape(NT2, P).T, "ones": ones, "counters": counters,
    }
    for f in range(FIELDS):
        arrays[f"tbl_{f}"] = a[f"tbl_{f}"]
    arrays = {k: np.ascontiguousarray(v) for k, v in arrays.items()}
    ap = {k: nc.dram_tensor(f"in_{k}", v.shape, mybir.dt.from_np(v.dtype), kind="ExternalInput").ap()
          for k, v in arrays.items()}
    out = nc.dram_tensor("out_y", (P, CHUNKS), mybir.dt.float32, kind="ExternalOutput").ap()
    dlrm_tower(nc, ap["ids_rows"], ap["ids_slots"], ap["dense_t"], [ap[f"tbl_{f}"] for f in range(FIELDS)],
               ap["W1"], ap["b1"], ap["W2"], ap["b2"], ap["W3"], ap["ones"], ap["counters"], out)
    r = _run(nc, [{f"in_{k}": v for k, v in arrays.items()}], core_ids=[0])
    return r.results[0]["out_y"].reshape(BATCH, 1)
```

```python
from contextlib import ExitStack

import concourse.bass as bass
import numpy as np
from concourse import mybir

P = 128
BATCH, FIELDS, DIM = 2048, 32, 64
VOCAB = [1000, 12500, 125000, 1250, 12500, 1250, 1250, 1000, 1000, 1250, 12500, 1250, 125000, 1000, 125000, 1000,
         1250, 1250, 1000, 1000, 1000, 1250, 1250, 12500, 1000, 1250, 1000, 1000, 12500, 12500, 1000, 1250]
GATHERED = [f for v in (125000, 12500) for f in range(FIELDS) if VOCAB[f] == v]
SMALL = [f for v in (1250, 1000) for f in range(FIELDS) if VOCAB[f] == v]
NG = len(GATHERED)
DENSE = 16
PAIRS = [(i, j) for i in range(FIELDS - 1) for j in range(i + 1, FIELDS)]
H1, H2 = 512, 256

CHUNKS = BATCH // P
TILE_CHUNKS = 2
TB = TILE_CHUNKS * P
TILES = BATCH // TB
TURNS = TILES // 2

PACKS, STRIPS = 6, 4
SLOTS = PACKS * STRIPS
STRIP = P // STRIPS
BLOCKS = 125
ROWS = [10, 10, 8, 8]
RMAX = max(ROWS)
PARTS = 3
TABLE = []
for vocab in (1250, 1000):
    own = [f for f in SMALL if VOCAB[f] == vocab]
    TABLE += own + [None] * (SLOTS // 2 - len(own))
PAIRS_OF_PACKS = PACKS // 2
NUMBERS = SLOTS * BATCH // P
HALF = SLOTS // 2 * TB
PLACE = {f: n for n, f in enumerate(GATHERED + SMALL)}
SUMROWS = PARTS * FIELDS

KT = H1 // P
NT2 = H2 // P
PAIR_ROWS_LAST = len(PAIRS) - (KT - 1) * P

GATHERS = NG * TILE_CHUNKS
GROUPS = 3
PER_GROUP = GATHERS // GROUPS
BROADCASTS = STRIPS + STRIPS

ROUND = 12582912.0


BF16_ONE = np.uint16(0x3F80)


def constants():
    sum_rows = np.zeros((P, PACKS, SUMROWS))
    row_in_block = np.full(P, -1.0)
    for g in range(STRIPS):
        for part in range(PARTS):
            for r in range(ROWS[g]):
                p = g * STRIP + part * RMAX + r
                row_in_block[p] = r
                for q in range(PACKS):
                    if TABLE[g * PACKS + q] is not None:
                        sum_rows[p, q, part * FIELDS + PLACE[TABLE[g * PACKS + q]]] = 1
    pair = np.zeros((P, KT, 2, P))
    for n, ij in enumerate(PAIRS):
        for side in range(2):
            for part in range(PARTS):
                pair[part * FIELDS + PLACE[ij[side]], n // P, side, n % P] = 1
    ones = np.concatenate([sum_rows.reshape(P, -1), pair.reshape(P, -1), np.eye(P)], axis=1)
    rows = np.repeat([ROWS[0], ROWS[-1]], P // 2)
    counters = np.stack([np.arange(P), row_in_block, 1.0 / rows, -rows], axis=1).astype(np.float32)
    return ones.astype(np.uint16) * BF16_ONE, counters


def dlrm_tower(nc, ids_rows, ids_slots, dense_t, small_tables, tables, W1, b1, W2, b2, W3, ones, counters, out):
    fp32, bf16, i32 = mybir.dt.float32, mybir.dt.bfloat16, mybir.dt.int32
    small = mybir.dt.uint8
    ALU, ACT, AX = mybir.AluOpType, mybir.ActivationFunctionType, mybir.AxisListType

    ctx = ExitStack()
    with ctx:
        def sb(name, shape, dt):
            return ctx.enter_context(nc.sbuf_tensor(name, shape, dt))

        def pb(name):
            return ctx.enter_context(nc.psum_tensor(name, [P, 512], fp32))

        def sem(name):
            return ctx.enter_context(nc.semaphore(name))

        ones_sb = sb("ones_sb", list(ones.shape), bf16)
        sel_rows = ones_sb[:, 0:PACKS * SUMROWS].rearrange("p (q m) -> p q m", q=PACKS)
        sel_pair = ones_sb[0:SUMROWS, PACKS * SUMROWS:PACKS * SUMROWS + KT * 2 * P].rearrange(
            "p (k s m) -> p k s m", k=KT, s=2)
        ident = ones_sb[:, PACKS * SUMROWS + KT * 2 * P:]
        count_sb = sb("count_sb", [P, 4], fp32)
        block_of_p, row_of_p, inverse_of_p, minus_rows_of_p = [count_sb[:, n:n + 1] for n in range(4)]
        W1_sb = sb("W1_sb", [P, KT, H1], fp32)
        W2_sb = sb("W2_sb", [P, KT, H2], fp32)
        W3_sb = sb("W3_sb", [P, NT2], fp32)
        b1_sb = sb("b1_sb", [P, KT], fp32)
        b2_sb = sb("b2_sb", [P, NT2], fp32)
        rows = sb("rows", [P, PACKS, sum(ROWS) * DIM], fp32)
        sums = sb("sums", [P, SLOTS, RMAX], fp32)
        rest = sb("rest", [P, 2, SLOTS, RMAX], fp32)
        sum_parts = sb("sum_parts", [P, SLOTS, STRIP], bf16)
        number = sb("number", [P, NUMBERS], i32)
        scaled = sb("scaled", [P, NUMBERS], fp32)
        block = sb("block", [P, NUMBERS], fp32)
        block_small = sb("block_small", [P, NUMBERS], small)
        row_small = sb("row_small", [P, NUMBERS], small)
        blocks_dram = nc.dram_tensor("blocks_dram", [2, TILES, HALF], small).ap()
        row_dram = nc.dram_tensor("row_dram", [2, TILES, HALF], small).ap()
        block_all = sb("block_all", [P, 2, SLOTS * TB], small)
        row_all = sb("row_all", [P, 2, PACKS, TB], small)
        onehot = sb("onehot", [P, 2, SLOTS, TB], bf16)
        picked = sb("picked", [P, 2, PACKS, TB], bf16)
        index = sb("index", [P, 2, TILE_CHUNKS, FIELDS], i32)
        gathered = sb("gathered", [P, 2, GATHERS, DIM], fp32)
        gsum = sb("gsum", [P, 2, NG, TILE_CHUNKS], fp32)
        grest = sb("grest", [P, 2, 2, NG, TILE_CHUNKS], fp32)
        gparts = sb("gparts", [P, 2, TILE_CHUNKS, PARTS, FIELDS], bf16)
        sums_t = sb("sums_t", [SUMROWS, 2, TB], bf16)
        right = sb("right", [P, 2, 2, TB], fp32)
        z = sb("z", [P, 2, KT, TB], fp32)
        h1 = sb("h1", [P, KT, TB], fp32)
        h2 = sb("h2", [P, NT2, TB], fp32)
        y_all = sb("y_all", [P, CHUNKS], fp32)

        ps_look = [pb("ps_look0"), pb("ps_look1")]
        ps_s = pb("ps_s")
        ps_left, ps_right = pb("ps_left"), pb("ps_right")
        ps_h1 = [pb("ps_h1a"), pb("ps_h1b")]
        ps_h2 = pb("ps_h2")
        ps_sum = ps_s[0:SUMROWS, 0:TB]
        ps_second = [ps_h2[:, 0:TB], ps_h1[0][:, 0:TB]]
        ps_y = ps_h1[1][:, 0:TILE_CHUNKS]

        ids_in = sem("ids_in")
        const_in = sem("const_in")
        count_in = sem("count_in")
        weights_in = sem("weights_in")
        bias_in = sem("bias_in")
        table_in = [sem(f"table_in{s}") for s in range(SLOTS)]
        blocks_found = sem("blocks_found")
        blocks_stored = sem("blocks_stored")
        broadcast_in = [sem(f"broadcast_in{b}") for b in range(2)]
        index_in = [sem(f"index_in{b}") for b in range(2)]
        dense_in = [sem(f"dense_in{b}") for b in range(2)]
        gather_in = [[sem(f"gather_in{b}{g}") for g in range(GROUPS)] for b in range(2)]
        dve_step = sem("dve_step")
        tables_split = sem("tables_split")
        onehot_built = sem("onehot_built")
        looked_up = sem("looked_up")
        row_picked = sem("row_picked")
        gather_summed = sem("gather_summed")
        gather_split = sem("gather_split")
        sums_in_psum = sem("sums_in_psum")
        sums_copied = sem("sums_copied")
        pairs_in_psum = sem("pairs_in_psum")
        right_copied = sem("right_copied")
        z_ready = sem("z_ready")
        h1_in_psum = sem("h1_in_psum")
        h1_ready = sem("h1_ready")
        h2_in_psum = sem("h2_in_psum")
        h2_ready = sem("h2_ready")
        y_in_psum = sem("y_in_psum")
        y_free = sem("y_free")
        out_written = sem("out_written")

        def slots_of(q):
            return [s for s in range(q, SLOTS, PACKS) if TABLE[s] is not None]

        def columns(s):
            g = s // PACKS
            return slice(sum(ROWS[:g]) * DIM, sum(ROWS[:g + 1]) * DIM)

        def load_pack(eng, q):
            for s in slots_of(q):
                eng.dma_start(rows[:, q, columns(s)], small_tables[q, :, columns(s)]).then_inc(table_in[s], 16)

        bl = ctx.enter_context(nc.Block())

        @bl.sync
        def _(sp):
            W = PACKS * TB

            def load_tile(t, b):
                for g in range(STRIPS):
                    sp.dma_start(block_all[:, b, g * W:(g + 1) * W],
                                 blocks_dram[g // 2, bass.ds(t, 1), g % 2 * W:(g % 2 + 1) * W].broadcast_to([P, W])
                                 ).then_inc(broadcast_in[b], 16)

            def load_rows(t, b):
                for g in range(STRIPS):
                    sp.dma_start(row_all[g * STRIP:(g + 1) * STRIP, b, :, :].rearrange("p q n -> p (q n)"),
                                 row_dram[g // 2, bass.ds(t, 1), g % 2 * W:(g % 2 + 1) * W].broadcast_to([STRIP, W])
                                 ).then_inc(broadcast_in[b], 16)

            def load_index(t, b):
                sp.dma_start(index[:, b, :, :], ids_rows[:, bass.ds(t * TILE_CHUNKS, TILE_CHUNKS), :]
                             ).then_inc(index_in[b], 16)

            def load_dense(t, b):
                sp.dma_start(z[PAIR_ROWS_LAST:P, b, KT - 1, :], dense_t[:, bass.ds(t * TB, TB)]
                             ).then_inc(dense_in[b], 16)

            sp.dma_start(number[:, :], ids_slots).then_inc(ids_in, 16)
            load_index(0, 0)
            sp.dma_start(count_sb[:, :], counters).then_inc(count_in, 16)
            load_index(1, 1)
            load_pack(sp, 0)
            sp.wait_ge(blocks_found, 2)
            sp.dma_start(blocks_dram.rearrange("h t n -> (h t n)").rearrange("(p x) -> p x", p=P), block_small[:, :]
                         ).then_inc(blocks_stored, 16)
            sp.dma_start(row_dram.rearrange("h t n -> (h t n)").rearrange("(p x) -> p x", p=P), row_small[:, :]
                         ).then_inc(blocks_stored, 16)
            load_pack(sp, 1)
            sp.wait_ge(blocks_stored, 32)
            load_tile(0, 0)
            load_rows(0, 0)
            for q in range(2, PACKS):
                load_pack(sp, q)
            load_dense(0, 0)
            for k in range(KT):
                sp.dma_start(W1_sb[:, k, :], W1[k * P:(k + 1) * P, :]).then_inc(weights_in, 16)
            load_tile(1, 1)
            load_rows(1, 1)
            load_dense(1, 1)
            sp.dma_start(W2_sb[:, :, :], W2.rearrange("(k p) n -> p k n", p=P)).then_inc(weights_in, 16)
            with sp.Fori(0, TURNS - 1) as turn:
                for b in range(2):
                    t = turn * 2 + b
                    sp.wait_ge(onehot_built, t + 1)
                    load_tile(t + 2, b)
                    sp.wait_ge(row_picked, t * PAIRS_OF_PACKS + PAIRS_OF_PACKS)
                    load_rows(t + 2, b)
                    sp.wait_ge(gather_summed, t * GROUPS + GROUPS)
                    load_index(t + 2, b)
                    sp.wait_ge(h1_in_psum, t * 2 + 2)
                    load_dense(t + 2, b)
            sp.wait_ge(y_free, TILES + 1)
            sp.dma_start(out, y_all[:, :]).then_inc(out_written, 16)
            sp.wait_ge(out_written, 16)

        @bl.gpsimd
        def _(pool):
            for t in range(TILES):
                b = t % 2
                pool.wait_ge(index_in[b], 16 * (t // 2 + 1))
                for n in range(GATHERS):
                    f, c = divmod(n, TILE_CHUNKS)
                    if t >= 2 and n % PER_GROUP == 0:
                        pool.wait_ge(gather_summed, (t - 2) * GROUPS + n // PER_GROUP + 1)
                    pool.indirect_dma_start(
                        gathered[:, b, n, :], None, tables[GATHERED[f]],
                        bass.IndirectOffsetOnAxis(index[:, b, c, GATHERED[f]:GATHERED[f] + 1], 0)
                    ).then_inc(gather_in[b][n // PER_GROUP], 16)

        @bl.scalar
        def _(act):
            act.wait_ge(table_in[0], 16)
            act.dma_start(ones_sb[:, :], ones.bitcast(bf16)).then_inc(const_in, 16)
            act.dma_start(b1_sb[:, :], b1).then_inc(bias_in, 16)
            act.dma_start(b2_sb[:, :], b2).then_inc(bias_in, 16)
            act.dma_start(W3_sb[:, :], W3).then_inc(weights_in, 16)

            act.wait_ge(bias_in, 32)
            act.nop().then_inc(y_free, 1)

            def copy_sums(t, b):
                act.wait_ge(sums_in_psum, t + 1)
                act.activation(sums_t[:, b, :], ps_sum, ACT.Copy).then_inc(sums_copied, 1)

            def copy_right(t, half):
                act.wait_ge(pairs_in_psum, t * 2 + half + 1)
                act.activation(right[:, half, :, :].rearrange("p k n -> p (k n)"), ps_right[:, :], ACT.Copy
                               ).then_inc(right_copied, 1)

            def second_units(t, k):
                act.wait_ge(h2_in_psum, t * NT2 + k + 1)
                act.activation(h2[:, k, :], ps_second[k], ACT.Relu, bias=b2_sb[:, k:k + 1]).then_inc(h2_ready, 1)

            def tile(t, b, more):
                for k in range(KT):
                    if k % 2 == 0:
                        act.wait_ge(h1_in_psum, t * 2 + k // 2 + 1)
                    act.activation(h1[:, k, :], ps_h1[k // 2][:, k % 2 * TB:(k % 2 + 1) * TB], ACT.Relu,
                                   bias=b1_sb[:, k:k + 1]).then_inc(h1_ready, 1)
                if more:
                    copy_sums(t + 1, 1 - b)
                for k in range(NT2):
                    second_units(t, k)
                    if more:
                        copy_right(t + 1, k)
                act.wait_ge(y_in_psum, t + 1)
                act.activation(y_all[:, bass.ds(t * TILE_CHUNKS, TILE_CHUNKS)], ps_y, ACT.Copy
                               ).then_inc(y_free, 1)

            copy_sums(0, 0)
            for half in range(2):
                copy_right(0, half)
            with act.Fori(0, TURNS - 1) as turn:
                for b in range(2):
                    tile(turn * 2 + b, b, True)
            for b in range(2):
                tile(TILES - 2 + b, b, b == 0)

        @bl.vector
        def _(dve):
            steps = [0]
            SPLIT_STEPS = 4

            def step(instruction, base=0):
                steps[0] += 1
                instruction.then_inc(dve_step, 1)
                dve.wait_ge(dve_step, base + steps[0])

            def split(parts, value, left, base=0):
                step(dve.tensor_copy(parts[0], value), base)
                step(dve.tensor_tensor(left[0], value, parts[0], ALU.subtract), base)
                step(dve.tensor_copy(parts[1], left[0]), base)
                step(dve.tensor_tensor(left[1], left[0], parts[1], ALU.subtract), base)
                return dve.tensor_copy(parts[2], left[1])

            def build_onehot(t, b, arrivals):
                dve.wait_ge(broadcast_in[b], arrivals)
                dve.tensor_scalar(onehot[:, b, :, :].rearrange("p s n -> p (s n)"), block_all[:, b, :],
                                  block_of_p, None, ALU.is_equal).then_inc(onehot_built, 1)

            def pick_rows(t, b):
                for i in range(PAIRS_OF_PACKS):
                    dve.wait_ge(looked_up, t * PAIRS_OF_PACKS + i + 1)
                    dve.scalar_tensor_tensor(
                        picked[:, b, 2 * i:2 * i + 2, :].rearrange("p q n -> p (q n)"),
                        row_all[:, b, 2 * i:2 * i + 2, :].rearrange("p q n -> p (q n)"),
                        row_of_p, ps_look[i % 2][:, :], ALU.is_equal, ALU.mult).then_inc(row_picked, 1)

            def sum_gathered(t, b, base):
                for g in range(GROUPS):
                    dve.wait_ge(gather_in[b][g], (t + 2 - b) * 8 * PER_GROUP)
                    n = slice(g * PER_GROUP, (g + 1) * PER_GROUP)
                    dve.tensor_reduce(gsum[:, b, :, :].rearrange("p f c -> p (f c)")[:, n],
                                      gathered[:, b, n, :], AX.X, ALU.add).then_inc(gather_summed, 1)
                dve.wait_ge(gather_summed, t * GROUPS + GROUPS)
                split([gparts[:, b, :, k, 0:NG].rearrange("p c f -> p f c") for k in range(PARTS)],
                      gsum[:, b, :, :], [grest[:, b, k, :, :] for k in range(2)], base).then_inc(gather_split, 1)

            def multiply_pairs(t, b):
                dve.wait_ge(right_copied, t * 2 + 1)
                dve.tensor_tensor(z[:, b, 0:2, :].rearrange("p k n -> p (k n)"), ps_left[:, :],
                                  right[:, 0, :, :].rearrange("p k n -> p (k n)"), ALU.mult).then_inc(z_ready, 1)
                dve.wait_ge(right_copied, t * 2 + 2)
                dve.tensor_tensor(z[:, b, 2, :], ps_left[:, 0:TB], right[:, 1, 0, :], ALU.mult
                                  ).then_inc(z_ready, 1)
                dve.tensor_tensor(z[0:PAIR_ROWS_LAST, b, 3, :], ps_left[0:PAIR_ROWS_LAST, TB:2 * TB],
                                  right[0:PAIR_ROWS_LAST, 1, 1, :], ALU.mult).then_inc(z_ready, 1)

            dve.wait_ge(ids_in, 16)
            dve.wait_ge(count_in, 16)
            step(dve.tensor_scalar(scaled[:, :], number[:, :], inverse_of_p, -0.45, ALU.mult, ALU.add))
            step(dve.tensor_scalar(block[:, :], scaled[:, :], ROUND, -ROUND, ALU.add, ALU.add))
            dve.tensor_copy(block_small[:, :], block[:, :]).then_inc(blocks_found, 1)
            dve.scalar_tensor_tensor(row_small[:, :], block[:, :], minus_rows_of_p, number[:, :], ALU.mult, ALU.add
                                     ).then_inc(blocks_found, 1)
            dve.memset(sum_parts[:, :, :], 0.0).then_inc(dve_step, 1)
            dve.memset(gparts[:, :, :, :, :], 0.0).then_inc(dve_step, 1)
            dve.memset(sums[:, :, :], 0.0).then_inc(dve_step, 1)
            steps[0] += 3
            dve.wait_ge(dve_step, steps[0])
            for i in range(PAIRS_OF_PACKS):
                for q in (2 * i, 2 * i + 1):
                    for s in slots_of(q):
                        dve.wait_ge(table_in[s], 16)
                        dve.tensor_reduce(sums[:, s, 0:ROWS[s // PACKS]],
                                          rows[:, q, columns(s)].rearrange("p (r d) -> p r d", d=DIM),
                                          AX.X, ALU.add).then_inc(dve_step, 1)
                        steps[0] += 1
                dve.wait_ge(dve_step, steps[0])

                def of_pair(x):
                    return x.rearrange("p (g q) r -> p g q r", g=STRIPS)[:, :, 2 * i:2 * i + 2, :]

                split([of_pair(sum_parts[:, :, k * RMAX:(k + 1) * RMAX]) for k in range(PARTS)],
                      of_pair(sums[:, :, :]), [of_pair(rest[:, k, :, :]) for k in range(2)]).then_inc(tables_split, 1)
                if i == 0:
                    build_onehot(0, 0, 16 * BROADCASTS)
            sum_gathered(0, 0, 0)
            pick_rows(0, 0)
            multiply_pairs(0, 0)
            build_onehot(1, 1, 16 * BROADCASTS)
            pick_rows(1, 1)
            sum_gathered(1, 1, 0)

            before = steps[0]
            with dve.Fori(0, TURNS - 1) as turn:
                for b in range(2):
                    t = turn * 2 + b
                    steps[0] = before
                    build_onehot(t + 2, b, (turn + 2) * 16 * BROADCASTS)
                    multiply_pairs(t + 1, 1 - b)
                    pick_rows(t + 2, b)
                    sum_gathered(t + 2, b, t * SPLIT_STEPS)
            multiply_pairs(TILES - 1, 1)

        @bl.tensor
        def _(pe):
            def look_up(t, b, i):
                for q in (2 * i, 2 * i + 1):
                    for g in range(STRIPS):
                        s = g * PACKS + q
                        last = pe.matmul(ps_look[i % 2][g * STRIP:(g + 1) * STRIP, q % 2 * TB:(q % 2 + 1) * TB],
                                         sum_parts[:, s, :], onehot[:, b, s, :], start=True, stop=True,
                                         tile_position=(0, g * STRIP))
                last.then_inc(looked_up, 1)

            def look_up_tile(t, b):
                pe.wait_ge(onehot_built, t + 1)
                for i in range(PAIRS_OF_PACKS):
                    if i == PAIRS_OF_PACKS - 1:
                        pe.wait_ge(row_picked, t * PAIRS_OF_PACKS + 1)
                    look_up(t, b, i)

            def transposed_sums(t, b):
                pe.wait_ge(row_picked, t * PAIRS_OF_PACKS + PAIRS_OF_PACKS)
                for q in range(PACKS):
                    pe.matmul(ps_sum, sel_rows[:, q, :], picked[:, b, q, :], start=(q == 0), stop=False)
                pe.wait_ge(gather_split, t + 1)
                for c in range(TILE_CHUNKS):
                    last = pe.matmul(ps_sum[:, c * P:(c + 1) * P],
                                     gparts[:, b, c, :, :].rearrange("p k f -> p (k f)"), ident,
                                     start=False, stop=(c == TILE_CHUNKS - 1))
                last.then_inc(sums_in_psum, 1)

            def pair_factors(t, b, half):
                if half == 0:
                    pe.wait_ge(sums_copied, t + 1)
                else:
                    pe.wait_ge(z_ready, t * 3 + 1)
                for k in range(2):
                    for side, ps in enumerate((ps_left, ps_right)):
                        last = pe.matmul(ps[:, k * TB:(k + 1) * TB], sel_pair[:, 2 * half + k, side, :],
                                         sums_t[:, b, :], start=True, stop=True)
                last.then_inc(pairs_in_psum, 1)

            def tile(t, b, prepare, look):
                pe.wait_ge(dense_in[b], (t + 2 - b) * 8)
                pe.wait_ge(z_ready, t * 3 + 3)
                for n in range(KT):
                    if n == 2:
                        pe.wait_ge(y_free, t + 1)
                    for k in range(KT):
                        last = pe.matmul(ps_h1[n // 2][:, n % 2 * TB:(n % 2 + 1) * TB],
                                         W1_sb[:, k, n * P:(n + 1) * P], z[:, b, k, :],
                                         start=(k == 0), stop=(k == KT - 1))
                    if n % 2:
                        last.then_inc(h1_in_psum, 1)
                if prepare:
                    transposed_sums(t + 1, 1 - b)
                for n in range(NT2):
                    for k in range(KT):
                        if n == 0:
                            pe.wait_ge(h1_ready, t * KT + k + 1)
                        last = pe.matmul(ps_second[n], W2_sb[:, k, n * P:(n + 1) * P], h1[:, k, :],
                                         start=(k == 0), stop=(k == KT - 1))
                    last.then_inc(h2_in_psum, 1)
                    if prepare:
                        pair_factors(t + 1, 1 - b, n)
                if look:
                    look_up_tile(t + 2, b)
                pe.wait_ge(h2_ready, t * NT2 + NT2)
                for c in range(TILE_CHUNKS):
                    for k in range(NT2):
                        last = pe.matmul(ps_y[:, c:c + 1], h2[:, k, c * P:(c + 1) * P], W3_sb[:, k:k + 1],
                                         start=(k == 0), stop=(k == NT2 - 1))
                last.then_inc(y_in_psum, 1)

            pe.wait_ge(const_in, 16)
            pe.wait_ge(onehot_built, 1)
            for i in range(PAIRS_OF_PACKS):
                pe.wait_ge(tables_split, i + 1)
                if i == PAIRS_OF_PACKS - 1:
                    pe.wait_ge(row_picked, 1)
                look_up(0, 0, i)
            transposed_sums(0, 0)
            for half in range(2):
                pair_factors(0, 0, half)
            look_up_tile(1, 1)
            pe.wait_ge(weights_in, 16 * (KT + 2))
            with pe.Fori(0, TURNS - 1) as turn:
                for b in range(2):
                    tile(turn * 2 + b, b, True, True)
            for b in range(2):
                tile(TILES - 2 + b, b, b == 0, False)


def kernel(**inputs):
    import concourse.bacc as _bacc
    from concourse.bass_utils import run_bass_kernel_spmd as _run

    nc = _bacc.Bacc("TRN2", target_bir_lowering=False, num_devices=1)
    a = {k: np.ascontiguousarray(v) for k, v in inputs.items()}
    ids = a["ids"].reshape(P, CHUNKS, FIELDS)
    by_slot = ids[:, :, [SMALL[0] if f is None else f for f in TABLE]]
    by_slot = by_slot.reshape(P, TILES, TILE_CHUNKS, 2, SLOTS // 2).transpose(3, 1, 4, 2, 0)
    ones, counters = constants()
    packed = np.zeros((PACKS, P, sum(ROWS) * DIM), np.float32)
    for s, f in enumerate(TABLE):
        g, q = divmod(s, PACKS)
        if f is not None:
            packed[q, :BLOCKS, sum(ROWS[:g]) * DIM:sum(ROWS[:g + 1]) * DIM] = a[f"tbl_{f}"].reshape(BLOCKS, -1)
    arrays = {
        "ids_rows": ids,
        "small_tables": packed,
        "ids_slots": by_slot.reshape(P, NUMBERS),
        "dense_t": a["dense_ctx"].reshape(P, CHUNKS, DENSE).transpose(2, 1, 0).reshape(DENSE, BATCH),
        "W1": a["W_top1"], "b1": a["b_top1"].reshape(KT, P).T,
        "W2": a["W_top2"], "b2": a["b_top2"].reshape(NT2, P).T,
        "W3": a["W_top3"].reshape(NT2, P).T, "ones": ones, "counters": counters,
    }
    for f in GATHERED:
        arrays[f"tbl_{f}"] = a[f"tbl_{f}"]
    arrays = {k: np.ascontiguousarray(v) for k, v in arrays.items()}
    ap = {k: nc.dram_tensor(f"in_{k}", v.shape, mybir.dt.from_np(v.dtype), kind="ExternalInput").ap()
          for k, v in arrays.items()}
    out = nc.dram_tensor("out_y", (P, CHUNKS), mybir.dt.float32, kind="ExternalOutput").ap()
    dlrm_tower(nc, ap["ids_rows"], ap["ids_slots"], ap["dense_t"], ap["small_tables"],
               {f: ap[f"tbl_{f}"] for f in GATHERED},
               ap["W1"], ap["b1"], ap["W2"], ap["b2"], ap["W3"], ap["ones"], ap["counters"], out)
    r = _run(nc, [{f"in_{k}": v for k, v in arrays.items()}], core_ids=[0])
    return r.results[0]["out_y"].reshape(BATCH, 1)
```

```python
from contextlib import ExitStack

import concourse.bass as bass
import numpy as np
from concourse import mybir

P = 128
BATCH, FIELDS, DIM = 2048, 32, 64
VOCAB = [1000, 12500, 125000, 1250, 12500, 1250, 1250, 1000, 1000, 1250, 12500, 1250, 125000, 1000, 125000, 1000,
         1250, 1250, 1000, 1000, 1000, 1250, 1250, 12500, 1000, 1250, 1000, 1000, 12500, 12500, 1000, 1250]
GATHERED = [f for v in (125000, 12500) for f in range(FIELDS) if VOCAB[f] == v]
SMALL = [f for v in (1250, 1000) for f in range(FIELDS) if VOCAB[f] == v]
NG = len(GATHERED)
SCANNED = GATHERED[-1]
SCAN_ROWS = VOCAB[SCANNED] // 125
FIRST_SCANNED = 2
DENSE = 16
PAIRS = [(i, j) for i in range(FIELDS - 1) for j in range(i + 1, FIELDS)]
H1, H2 = 512, 256

CHUNKS = BATCH // P
TILE_CHUNKS = 2
TB = TILE_CHUNKS * P
TILES = BATCH // TB
TURNS = TILES // 2

PACKS, STRIPS = 6, 4
SLOTS = PACKS * STRIPS
STRIP = P // STRIPS
BLOCKS = 125
ROWS = [10, 10, 8, 8]
RMAX = max(ROWS)
PARTS = 3
TABLE = []
for vocab in (1250, 1000):
    own = [f for f in SMALL if VOCAB[f] == vocab]
    TABLE += own + [None] * (SLOTS // 2 - len(own))
PAIRS_OF_PACKS = PACKS // 2
DVE_PACKS = 4
ACT_PACKS = PACKS - DVE_PACKS
NUMBERS = SLOTS * BATCH // P
HALF = SLOTS // 2 * TB
PLACE = {f: n for n, f in enumerate(GATHERED + SMALL)}
SUMROWS = PARTS * FIELDS

KT = H1 // P
NT2 = H2 // P
PAIR_ROWS_LAST = len(PAIRS) - (KT - 1) * P

GATHERS = NG * TILE_CHUNKS
GROUPS = 3
PER_GROUP = GATHERS // GROUPS
LATER_GATHERS = GATHERS - TILE_CHUNKS
LATER_LAST = PER_GROUP - TILE_CHUNKS
BROADCASTS = STRIPS + STRIPS
SCAN_CHUNKS = 4
SCAN_PIECES = [(0, 112), (112, 13)]

ROUND = 12582912.0


BF16_ONE = np.uint16(0x3F80)


def constants():
    sum_rows = np.zeros((P, PACKS, SUMROWS))
    row_in_block = np.full(P, -1.0)
    for g in range(STRIPS):
        for part in range(PARTS):
            for r in range(ROWS[g]):
                p = g * STRIP + part * RMAX + r
                row_in_block[p] = r
                for q in range(PACKS):
                    if TABLE[g * PACKS + q] is not None:
                        sum_rows[p, q, part * FIELDS + PLACE[TABLE[g * PACKS + q]]] = 1
    pair = np.zeros((P, KT, 2, P))
    for n, ij in enumerate(PAIRS):
        for side in range(2):
            for part in range(PARTS):
                pair[part * FIELDS + PLACE[ij[side]], n // P, side, n % P] = 1
    scan = np.zeros((P, PARTS, SUMROWS))
    for part in range(PARTS):
        scan[:SCAN_ROWS, part, part * FIELDS + PLACE[SCANNED]] = 1
    ones = np.concatenate([scan.reshape(P, -1), sum_rows.reshape(P, -1), pair.reshape(P, -1), np.eye(P)], axis=1)
    rows = np.repeat([ROWS[0], ROWS[-1]], P // 2)
    counters = np.stack([np.arange(P), row_in_block, 1.0 / rows, -rows, -np.arange(P), np.ones(P)], axis=1)
    return ones.astype(np.uint16) * BF16_ONE, counters.astype(np.float32)


def dlrm_tower(nc, ids_rows, ids_slots, ids_scan, dense_t, small_tables, tables, W1, b1, W2, b2, W3, ones, counters,
               out):
    fp32, bf16, i32 = mybir.dt.float32, mybir.dt.bfloat16, mybir.dt.int32
    small = mybir.dt.uint8
    ALU, ACT, AX = mybir.AluOpType, mybir.ActivationFunctionType, mybir.AxisListType

    ctx = ExitStack()
    with ctx:
        def sb(name, shape, dt):
            return ctx.enter_context(nc.sbuf_tensor(name, shape, dt))

        def pb(name):
            return ctx.enter_context(nc.psum_tensor(name, [P, 512], fp32))

        def sem(name):
            return ctx.enter_context(nc.semaphore(name))

        ones_sb = sb("ones_sb", list(ones.shape), bf16)
        ends = np.cumsum([PARTS * SUMROWS, PACKS * SUMROWS, KT * 2 * P, P]).tolist()
        sel_scan = ones_sb[0:SCAN_ROWS, 0:ends[0]].rearrange("p (k m) -> p k m", k=PARTS)
        sel_rows = ones_sb[:, ends[0]:ends[1]].rearrange("p (q m) -> p q m", q=PACKS)
        sel_pair = ones_sb[0:SUMROWS, ends[1]:ends[2]].rearrange("p (k s m) -> p k s m", k=KT, s=2)
        ident = ones_sb[:, ends[2]:ends[3]]
        count_sb = sb("count_sb", [P, 6], fp32)
        block_of_p, row_of_p, inverse_of_p, minus_rows_of_p, minus_block_of_p, one_of_p = [
            count_sb[:, n:n + 1] for n in range(6)]
        W1_sb = sb("W1_sb", [P, KT, H1], fp32)
        W2_sb = sb("W2_sb", [P, KT, H2], fp32)
        W3_sb = sb("W3_sb", [P, NT2], fp32)
        b1_sb = sb("b1_sb", [P, KT], fp32)
        b2_sb = sb("b2_sb", [P, NT2], fp32)
        rows = sb("rows", [P, PACKS, sum(ROWS) * DIM], fp32)
        sums = sb("sums", [P, SLOTS, RMAX], fp32)
        rest = sb("rest", [P, 2, SLOTS, RMAX], fp32)
        sum_parts = sb("sum_parts", [P, SLOTS, STRIP], bf16)
        number = sb("number", [P, NUMBERS], i32)
        scaled = sb("scaled", [P, NUMBERS], fp32)
        block = sb("block", [P, NUMBERS], fp32)
        block_small = sb("block_small", [P, NUMBERS], small)
        row_small = sb("row_small", [P, NUMBERS], small)
        scan_rows = rows[:, 0:3, :].rearrange("p q n -> p (q n)")[:, 0:SCAN_ROWS * DIM]
        scan_sums = sb("scan_sums", [P, SCAN_ROWS], fp32)
        scan_rest = sb("scan_rest", [P, 2, SCAN_ROWS], fp32)
        scan_parts = sb("scan_parts", [P, PARTS, SCAN_ROWS], bf16)
        scan_number = sb("scan_number", [P, CHUNKS], i32)
        scan_scaled = sb("scan_scaled", [P, CHUNKS], fp32)
        scan_block = sb("scan_block", [P, CHUNKS], fp32)
        scan_small = sb("scan_small", [P, 2, CHUNKS], small)
        scan_dram = nc.dram_tensor("scan_dram", [2, BATCH], small).ap()
        scan_all = sb("scan_all", [P, 2, BATCH], small)
        scan_onehot = sb("scan_onehot", [P, 2, TB], bf16)
        scan_picked = sb("scan_picked", [P, 2, PARTS, TB], bf16)
        blocks_dram = nc.dram_tensor("blocks_dram", [2, TILES, HALF], small).ap()
        row_dram = nc.dram_tensor("row_dram", [2, TILES, HALF], small).ap()
        index = sb("index", [P, CHUNKS, NG], i32)
        block_all = sb("block_all", [P, 2, SLOTS * TB], small)
        row_all = sb("row_all", [P, 2, PACKS, TB], small)
        onehot = sb("onehot", [P, 2, SLOTS, TB], bf16)
        distance = sb("distance", [P, 2, STRIPS, TB], bf16)
        picked = sb("picked", [P, 2, PACKS, TB], bf16)
        gathered = sb("gathered", [P, 2, GATHERS, DIM], fp32)
        gsum = sb("gsum", [P, 2, NG, TILE_CHUNKS], fp32)
        grest = sb("grest", [P, 2, 2, NG, TILE_CHUNKS], fp32)
        gparts = sb("gparts", [P, 2, TILE_CHUNKS, PARTS, FIELDS], bf16)
        sums_t = sb("sums_t", [SUMROWS, 2, TB], bf16)
        right = sb("right", [P, 2, 2, TB], fp32)
        z = sb("z", [P, 2, KT, TB], fp32)
        h1 = sb("h1", [P, KT, TB], fp32)
        h2 = sb("h2", [P, NT2, TB], fp32)
        h2_scaled = sb("h2_scaled", [P, TB], fp32)
        h2_total = sb("h2_total", [P, TB], fp32)
        y_all = sb("y_all", [1, BATCH], fp32)

        ps_look = [pb("ps_look0"), pb("ps_look1")]
        ps_s = pb("ps_s")
        ps_left, ps_right = pb("ps_left"), pb("ps_right")
        ps_h1 = [pb("ps_h1a"), pb("ps_h1b")]
        ps_h2 = pb("ps_h2")
        ps_sum = ps_s[0:SUMROWS, 0:TB]
        ps_y = ps_h1[1][0:1, 0:TB]
        ps_second = [ps_h2[:, 0:TB], ps_s[:, TB:2 * TB]]
        ps_second_late = [ps_h2[:, 0:TB], ps_look[0][:, 0:TB]]
        ps_y_late = ps_left[0:1, 0:TB]
        ps_y_chunk = [ps_right[0:1, 0:P], ps_left[0:1, TB:TB + P]]

        ids_in = sem("ids_in")
        const_in = sem("const_in")
        count_in = sem("count_in")
        first_weights_in = sem("first_weights_in")
        weights_in = sem("weights_in")
        bias_in = sem("bias_in")
        table_in = [sem(f"table_in{s}") for s in range(SLOTS)]
        blocks_found = sem("blocks_found")
        blocks_stored = sem("blocks_stored")
        broadcast_in = [sem(f"broadcast_in{b}") for b in range(2)]
        index_in = sem("index_in")
        dense_in = [sem(f"dense_in{b}") for b in range(2)]
        gather_in = [[sem(f"gather_in{b}{g}") for g in range(GROUPS)] for b in range(2)]
        dve_step = sem("dve_step")
        tables_split = sem("tables_split")
        onehot_built = sem("onehot_built")
        distances_found = sem("distances_found")
        act_onehot_built = sem("act_onehot_built")
        looked_up = sem("looked_up")
        row_picked = sem("row_picked")
        gather_summed = sem("gather_summed")
        scan_table_in = [sem(f"scan_table_in{k}") for k in range(SCAN_CHUNKS)]
        scan_numbers_in = sem("scan_numbers_in")
        scan_split = sem("scan_split")
        scan_onehot_built = sem("scan_onehot_built")
        scan_looked_up = sem("scan_looked_up")
        scan_row_picked = sem("scan_row_picked")
        gather_split = sem("gather_split")
        sums_in_psum = sem("sums_in_psum")
        sums_copied = sem("sums_copied")
        pairs_in_psum = sem("pairs_in_psum")
        right_copied = sem("right_copied")
        z_ready = sem("z_ready")
        h1_in_psum = sem("h1_in_psum")
        h1_ready = sem("h1_ready")
        h2_in_psum = sem("h2_in_psum")
        h2_ready = sem("h2_ready")
        h2_scaled_ready = sem("h2_scaled_ready")
        h2_total_ready = sem("h2_total_ready")
        y_in_psum = sem("y_in_psum")
        y_copied = sem("y_copied")
        out_written = sem("out_written")

        def packs_of(x, first, count):
            return x.rearrange("p (g n) -> p g n", g=STRIPS)[:, :, first * TB:(first + count) * TB]

        def slots_of(q):
            return [s for s in range(q, SLOTS, PACKS) if TABLE[s] is not None]

        def columns(s):
            g = s // PACKS
            return slice(sum(ROWS[:g]) * DIM, sum(ROWS[:g + 1]) * DIM)

        def load_pack(eng, q):
            for s in slots_of(q):
                eng.dma_start(rows[:, q, columns(s)], small_tables[q, :, columns(s)]).then_inc(table_in[s], 16)

        bl = ctx.enter_context(nc.Block())

        @bl.sync
        def _(sp):
            W = PACKS * TB

            def load_tile(t, b):
                for g in range(STRIPS):
                    sp.dma_start(block_all[:, b, g * W:(g + 1) * W],
                                 blocks_dram[g // 2, bass.ds(t, 1), g % 2 * W:(g % 2 + 1) * W].broadcast_to([P, W])
                                 ).then_inc(broadcast_in[b], 16)

            def load_rows(t, b):
                for g in range(STRIPS):
                    sp.dma_start(row_all[g * STRIP:(g + 1) * STRIP, b, :, :].rearrange("p q n -> p (q n)"),
                                 row_dram[g // 2, bass.ds(t, 1), g % 2 * W:(g % 2 + 1) * W].broadcast_to([STRIP, W])
                                 ).then_inc(broadcast_in[b], 16)

            def load_dense(t, b):
                sp.dma_start(z[PAIR_ROWS_LAST:P, b, KT - 1, :],
                             dense_t[bass.ds(t, 1), :, :].rearrange("o d n -> (o d) n")
                             ).then_inc(dense_in[b], 16)

            def load_numbers(t, b):
                sp.wait_ge(row_picked, t * PAIRS_OF_PACKS + PAIRS_OF_PACKS)
                load_tile(t + 2, b)
                load_rows(t + 2, b)

            def load_next_dense(t, b):
                sp.wait_ge(h1_in_psum, t * 2 + 2)
                load_dense(t + 2, b)

            def load_scanned(k):
                w = SCAN_ROWS // SCAN_CHUNKS * DIM
                for first, n in SCAN_PIECES:
                    sp.dma_start(scan_rows[first:first + n, k * w:(k + 1) * w],
                                 tables[SCANNED].rearrange("(p r) d -> p (r d)", r=SCAN_ROWS)[
                                     first:first + n, k * w:(k + 1) * w]).then_inc(scan_table_in[k], 16)

            sp.dma_start(index[:, :, :], ids_rows).then_inc(index_in, 16)
            sp.dma_start(number[:, :], ids_slots).then_inc(ids_in, 16)
            sp.dma_start(scan_number[:, :], ids_scan).then_inc(ids_in, 16)
            sp.dma_start(count_sb[:, :], counters).then_inc(count_in, 16)
            load_pack(sp, 0)
            sp.wait_ge(blocks_found, 4)
            sp.dma_start(blocks_dram.rearrange("h t n -> (h t n)").rearrange("(p x) -> p x", p=P), block_small[:, :]
                         ).then_inc(blocks_stored, 16)
            sp.dma_start(row_dram.rearrange("h t n -> (h t n)").rearrange("(p x) -> p x", p=P), row_small[:, :]
                         ).then_inc(blocks_stored, 16)
            sp.dma_start(scan_dram.rearrange("s (p x) -> p s x", p=P),
                         scan_small[:, :, :]).then_inc(blocks_stored, 16)
            load_pack(sp, 1)
            sp.wait_ge(blocks_stored, 48)
            load_tile(0, 0)
            load_rows(0, 0)
            for q in range(2, PACKS):
                load_pack(sp, q)
            sp.dma_start(ones_sb[:, :], ones.bitcast(bf16)).then_inc(const_in, 16)
            load_dense(0, 0)
            load_tile(1, 1)
            load_rows(1, 1)
            for k in range(KT):
                sp.dma_start(W1_sb[:, k, :], W1[k * P:(k + 1) * P, :]).then_inc(first_weights_in, 16)
            sp.dma_start(b1_sb[:, :], b1).then_inc(bias_in, 16)
            sp.dma_start(b2_sb[:, :], b2).then_inc(bias_in, 16)
            sp.dma_start(W3_sb[:, :], W3).then_inc(weights_in, 16)
            load_dense(1, 1)
            load_numbers(0, 0)
            sp.dma_start(W2_sb[:, :, :], W2.rearrange("(k p) n -> p k n", p=P)).then_inc(weights_in, 16)
            sp.wait_ge(tables_split, 2)
            sp.wait_ge(gather_in[1][GROUPS - 1], 16 * PER_GROUP)
            for k in range(SCAN_CHUNKS):
                load_scanned(k)
            sp.dma_start(scan_all[:, :, :], scan_dram.rearrange("(o s) n -> o s n", o=1).broadcast_to([P, 2, BATCH])
                         ).then_inc(scan_numbers_in, 16)
            load_numbers(1, 1)
            load_next_dense(0, 0)
            load_next_dense(1, 1)
            with sp.Fori(1, TURNS - 1) as turn:
                for b in range(2):
                    load_numbers(turn * 2 + b, b)
                    load_next_dense(turn * 2 + b, b)
            sp.wait_ge(y_copied, TILES + 1)
            sp.dma_start(out, y_all[:, :]).then_inc(out_written, 16)
            sp.wait_ge(out_written, 16)

        @bl.gpsimd
        def _(pool):
            pool.wait_ge(index_in, 16)
            for t in range(TILES):
                b = t % 2
                for n in range(GATHERS if t < FIRST_SCANNED else LATER_GATHERS):
                    f, c = divmod(n, TILE_CHUNKS)
                    if t == TILES - 1:
                        c, f = divmod(n, NG - 1)
                    if t >= 2 and n % PER_GROUP == 0:
                        pool.wait_ge(gather_summed, (t - 2) * GROUPS + n // PER_GROUP + 1)
                    pool.indirect_dma_start(
                        gathered[:, b, n, :], None, tables[GATHERED[f]],
                        bass.IndirectOffsetOnAxis(index[:, t * TILE_CHUNKS + c, f:f + 1], 0)
                    ).then_inc(gather_in[b][c if t == TILES - 1 else n // PER_GROUP], 16)

        @bl.scalar
        def _(act):
            def onehot_pack(b, q, count):
                act.activation(distance[:, q % 2, :, :], packs_of(block_all[:, b, :], q, 1), ACT.Square,
                               bias=minus_block_of_p).then_inc(distances_found, 1)
                act.wait_ge(distances_found, count + 1)
                act.activation(packs_of(onehot[:, b, :, :].rearrange("p s n -> p (s n)"), q, 1),
                               distance[:, q % 2, :, :], ACT.Relu, bias=one_of_p, scale=-1.0).then_inc(act_onehot_built, 1)

            def copy_sums(t, b):
                act.wait_ge(sums_in_psum, t + 1)
                act.activation(sums_t[:, b, :], ps_sum, ACT.Copy).then_inc(sums_copied, 1)

            def copy_right(t, half, ps):
                act.wait_ge(pairs_in_psum, t * 2 + half + 1)
                act.activation(right[:, half, :, :].rearrange("p k n -> p (k n)"), ps[:, :], ACT.Copy
                               ).then_inc(right_copied, 1)

            def second_units(t, k, ps):
                act.wait_ge(h2_in_psum, t * NT2 + k + 1)
                act.activation(h2[:, k, :], ps, ACT.Relu, bias=b2_sb[:, k:k + 1]).then_inc(h2_ready, 1)

            def prepare_apart(t, b):
                copy_sums(t, b)
                copy_right(t, 0, ps_right)
                copy_right(t, 1, ps_s)

            def copy_results(t):
                act.wait_ge(y_in_psum, t + 1)
                act.activation(y_all[:, bass.ds(t * TB, TB)], ps_y, ACT.Copy).then_inc(y_copied, 1)

            def tile(t, b, turn, prepare, look, first=False):
                packs_built = PACKS + (t + 1) * ACT_PACKS
                if not first:
                    copy_results(t - 1)
                if look:
                    act.wait_ge(broadcast_in[b], (turn + 2) * 16 * BROADCASTS)
                    onehot_pack(b, DVE_PACKS, packs_built + 1)
                for k in range(KT):
                    if k % 2 == 0:
                        act.wait_ge(h1_in_psum, t * 2 + k // 2 + 1)
                    act.activation(h1[:, k, :], ps_h1[k // 2][:, k % 2 * TB:(k % 2 + 1) * TB], ACT.Relu,
                                   bias=b1_sb[:, k:k + 1]).then_inc(h1_ready, 1)
                    if k == (1 if first else KT - 1) and prepare:
                        copy_sums(t + 1, 1 - b)
                    if k == 1 and look:
                        onehot_pack(b, DVE_PACKS + 1, packs_built + 2)
                if prepare:
                    for k in range(NT2):
                        copy_right(t + 1, k, ps_right)
                        second_units(t, k, ps_second[k])

            act.wait_ge(count_in, 16)
            act.activation(distance[:, 1, 0, 0:1], one_of_p, ACT.Square).then_inc(distances_found, 1)
            act.wait_ge(broadcast_in[0], 16 * BROADCASTS)
            for q in range(PACKS):
                onehot_pack(0, q, q + 1)
            act.wait_ge(broadcast_in[1], 16 * BROADCASTS)
            onehot_pack(1, DVE_PACKS, PACKS + 1)
            prepare_apart(0, 0)
            onehot_pack(1, DVE_PACKS + 1, PACKS + 2)
            act.wait_ge(bias_in, 32)
            tile(0, 0, 0, True, True, first=True)
            tile(1, 1, 0, True, True)
            with act.Fori(1, TURNS - 1) as turn:
                for b in range(2):
                    tile(turn * 2 + b, b, turn, True, True)
            tile(TILES - 2, 0, TURNS - 1, False, False)
            t, b = TILES - 1, 1
            halves = [slice(c * P, (c + 1) * P) for c in range(TILE_CHUNKS)]

            def chunk_sums(c):
                act.wait_ge(sums_in_psum, t + c + 1)
                act.activation(sums_t[:, b, halves[c]], ps_sum[:, halves[c]], ACT.Copy).then_inc(sums_copied, 1)

            def chunk_right(c, ps):
                act.wait_ge(pairs_in_psum, t * 2 + c + 1)
                act.activation(right[:, c, :, :].rearrange("p k n -> p (k n)"), ps[:, :], ACT.Copy
                               ).then_inc(right_copied, 1)

            def chunk_first_units(c, i):
                act.wait_ge(h1_in_psum, (t + c) * 2 + i + 1)
                for k in (2 * i, 2 * i + 1):
                    act.activation(h1[:, k, halves[c]], ps_h1[i][:, k % 2 * P:(k % 2 + 1) * P], ACT.Relu,
                                   bias=b1_sb[:, k:k + 1]).then_inc(h1_ready, 1)

            def chunk_second_units(c, k, ps):
                act.wait_ge(h2_in_psum, (t + c) * NT2 + k + 1)
                act.activation(h2[:, k, halves[c]], ps[:, 0:P], ACT.Relu, bias=b2_sb[:, k:k + 1]).then_inc(h2_ready, 1)

            def copy_y(count, first, ps, n):
                act.wait_ge(y_in_psum, count)
                act.activation(y_all[:, first:first + n], ps, ACT.Copy).then_inc(y_copied, 1)

            chunk_sums(0)
            second_units(t - 1, 0, ps_second_late[0])
            chunk_right(0, ps_right)
            second_units(t - 1, 1, ps_second_late[1])
            chunk_first_units(0, 0)
            chunk_sums(1)
            chunk_first_units(0, 1)
            copy_y(t, (t - 1) * TB, ps_y_late, TB)
            chunk_right(1, ps_look[1])
            chunk_second_units(0, 0, ps_h2)
            chunk_second_units(0, 1, ps_s)
            chunk_first_units(1, 0)
            chunk_first_units(1, 1)
            copy_y(t + 1, t * TB, ps_y_chunk[0], P)
            chunk_second_units(1, 0, ps_look[0])
            chunk_second_units(1, 1, ps_look[1])
            copy_y(t + 2, t * TB + P, ps_y_chunk[1], P)

        @bl.vector
        def _(dve):
            steps = [0]
            SPLIT_STEPS = 4

            def step(instruction, base=0):
                steps[0] += 1
                instruction.then_inc(dve_step, 1)
                dve.wait_ge(dve_step, base + steps[0])

            def split(parts, value, left, base=0):
                step(dve.tensor_copy(parts[0], value), base)
                step(dve.tensor_tensor(left[0], value, parts[0], ALU.subtract), base)
                step(dve.tensor_copy(parts[1], left[0]), base)
                step(dve.tensor_tensor(left[1], left[0], parts[1], ALU.subtract), base)
                return dve.tensor_copy(parts[2], left[1])

            def build_onehot(t, b, arrivals):
                dve.wait_ge(broadcast_in[b], arrivals)
                dve.tensor_scalar(packs_of(onehot[:, b, :, :].rearrange("p s n -> p (s n)"), 0, DVE_PACKS),
                                  packs_of(block_all[:, b, :], 0, DVE_PACKS),
                                  block_of_p, None, ALU.is_equal).then_inc(onehot_built, 1)

            def build_scan_onehot(t, b):
                dve.wait_ge(scan_numbers_in, 16)
                dve.tensor_scalar(scan_onehot[:, b, :], scan_all[:, 0, bass.ds(t * TB, TB)], block_of_p, None,
                                  ALU.is_equal).then_inc(scan_onehot_built, 1)

            def pick_rows(t, b, i):
                dve.wait_ge(looked_up, t * PAIRS_OF_PACKS + i + 1)
                dve.scalar_tensor_tensor(
                    picked[:, b, 2 * i:2 * i + 2, :].rearrange("p q n -> p (q n)"),
                    row_all[:, b, 2 * i:2 * i + 2, :].rearrange("p q n -> p (q n)"),
                    row_of_p, ps_look[i % 2][:, :], ALU.is_equal, ALU.mult).then_inc(row_picked, 1)

            def pick_scan_rows(t, b):
                for i, parts in enumerate((slice(0, 2), slice(2, 3))):
                    dve.wait_ge(scan_looked_up, (t - FIRST_SCANNED) * 2 + i + 1)
                    k = parts.stop - parts.start
                    dve.scalar_tensor_tensor(
                        scan_picked[0:SCAN_ROWS, b, parts, :],
                        scan_all[0:SCAN_ROWS, 1:2, bass.ds(t * TB, TB)].broadcast_to([SCAN_ROWS, k, TB]),
                        block_of_p[0:SCAN_ROWS, :],
                        ps_look[1 - i][0:SCAN_ROWS, 0:k * TB].rearrange("p (k n) -> p k n", k=k),
                        ALU.is_equal, ALU.mult).then_inc(scan_row_picked, 1)

            def sum_gathered(t, b, g, arrivals, count=PER_GROUP):
                dve.wait_ge(gather_in[b][g], arrivals)
                n = slice(g * PER_GROUP, g * PER_GROUP + count)
                dve.tensor_reduce(gsum[:, b, :, :].rearrange("p f c -> p (f c)")[:, n],
                                  gathered[:, b, n, :], AX.X, ALU.add).then_inc(gather_summed, 1)

            def split_gathered(t, b, base=0):
                dve.wait_ge(gather_summed, t * GROUPS + GROUPS)
                split([gparts[:, b, :, k, 0:NG].rearrange("p c f -> p f c") for k in range(PARTS)],
                      gsum[:, b, :, :], [grest[:, b, k, :, :] for k in range(2)], base).then_inc(gather_split, 1)

            def multiply_pairs(t, b, half, ps=ps_left):
                dve.wait_ge(right_copied, t * 2 + half + 1)
                if half == 0:
                    dve.tensor_tensor(z[:, b, 0:2, :].rearrange("p k n -> p (k n)"), ps[:, :],
                                      right[:, 0, :, :].rearrange("p k n -> p (k n)"), ALU.mult).then_inc(z_ready, 1)
                else:
                    dve.tensor_tensor(z[:, b, 2, :], ps[:, 0:TB], right[:, 1, 0, :], ALU.mult
                                      ).then_inc(z_ready, 1)
                    dve.tensor_tensor(z[0:PAIR_ROWS_LAST, b, 3, :], ps[0:PAIR_ROWS_LAST, TB:2 * TB],
                                      right[0:PAIR_ROWS_LAST, 1, 1, :], ALU.mult).then_inc(z_ready, 1)

            dve.wait_ge(ids_in, 32)
            dve.wait_ge(count_in, 16)
            step(dve.tensor_scalar(scaled[:, :], number[:, :], inverse_of_p, -0.45, ALU.mult, ALU.add))
            step(dve.tensor_scalar(block[:, :], scaled[:, :], ROUND, -ROUND, ALU.add, ALU.add))
            dve.tensor_copy(block_small[:, :], block[:, :]).then_inc(blocks_found, 1)
            dve.scalar_tensor_tensor(row_small[:, :], block[:, :], minus_rows_of_p, number[:, :], ALU.mult, ALU.add
                                     ).then_inc(blocks_found, 1)
            step(dve.tensor_scalar(scan_scaled[:, :], scan_number[:, :], 1.0 / SCAN_ROWS, -0.495, ALU.mult, ALU.add))
            step(dve.tensor_scalar(scan_block[:, :], scan_scaled[:, :], ROUND, -ROUND, ALU.add, ALU.add))
            dve.tensor_copy(scan_small[:, 0, :], scan_block[:, :]).then_inc(blocks_found, 1)
            dve.scalar_tensor_tensor(scan_small[:, 1, :], scan_block[:, :], -float(SCAN_ROWS), scan_number[:, :],
                                     ALU.mult, ALU.add).then_inc(blocks_found, 1)
            for b in range(2):
                dve.memset(scan_picked[:, b, :, :], 0.0).then_inc(scan_row_picked, 1)
            dve.memset(sum_parts[:, :, :], 0.0).then_inc(dve_step, 1)
            dve.memset(gparts[:, :, :, :, :], 0.0).then_inc(dve_step, 1)
            dve.memset(sums[:, :, :], 0.0).then_inc(dve_step, 1)
            steps[0] += 3
            dve.wait_ge(dve_step, steps[0])
            for i in range(PAIRS_OF_PACKS):
                for q in (2 * i, 2 * i + 1):
                    for s in slots_of(q):
                        dve.wait_ge(table_in[s], 16)
                        dve.tensor_reduce(sums[:, s, 0:ROWS[s // PACKS]],
                                          rows[:, q, columns(s)].rearrange("p (r d) -> p r d", d=DIM),
                                          AX.X, ALU.add).then_inc(dve_step, 1)
                        steps[0] += 1
                dve.wait_ge(dve_step, steps[0])

                def of_pair(x):
                    return x.rearrange("p (g q) r -> p g q r", g=STRIPS)[:, :, 2 * i:2 * i + 2, :]

                split([of_pair(sum_parts[:, :, k * RMAX:(k + 1) * RMAX]) for k in range(PARTS)],
                      of_pair(sums[:, :, :]), [of_pair(rest[:, k, :, :]) for k in range(2)]).then_inc(tables_split, 1)
                if i == 1:
                    pick_rows(0, 0, 0)
            pick_rows(0, 0, 1)
            pick_rows(0, 0, 2)
            for g in range(GROUPS):
                sum_gathered(0, 0, g, 16 * PER_GROUP)
            split_gathered(0, 0)
            build_onehot(1, 1, 16 * BROADCASTS)
            multiply_pairs(0, 0, 0)
            multiply_pairs(0, 0, 1, ps_h2)
            def sum_scanned(k):
                w = SCAN_ROWS // SCAN_CHUNKS
                dve.wait_ge(scan_table_in[k], 16 * len(SCAN_PIECES))
                step(dve.tensor_reduce(scan_sums[0:BLOCKS, k * w:(k + 1) * w],
                                       scan_rows[0:BLOCKS, k * w * DIM:(k + 1) * w * DIM].rearrange(
                                           "p (r d) -> p r d", d=DIM), AX.X, ALU.add))
                if k == SCAN_CHUNKS - 1:
                    split([scan_parts[0:BLOCKS, k, :] for k in range(PARTS)], scan_sums[0:BLOCKS, :],
                          [scan_rest[0:BLOCKS, k, :] for k in range(2)]).then_inc(scan_split, 1)

            pick_rows(1, 1, 0)
            pick_rows(1, 1, 1)
            build_onehot(2, 0, 2 * 16 * BROADCASTS)
            pick_rows(1, 1, 2)
            for g in range(GROUPS):
                sum_gathered(1, 1, g, 16 * PER_GROUP)
            split_gathered(1, 1)
            for b in range(2):
                step(dve.memset(gsum[:, b, NG - 1, :], 0.0))

            def weigh_units(t):
                dve.wait_ge(h2_ready, t * NT2 + NT2)
                dve.tensor_scalar(h2_scaled[:, :], h2[:, 0, :], W3_sb[:, 0:1], None, ALU.mult
                                  ).then_inc(h2_scaled_ready, 1)
                dve.wait_ge(h2_scaled_ready, t + 1)
                dve.scalar_tensor_tensor(h2_total[:, :], h2[:, 1, :], W3_sb[:, 1:2], h2_scaled[:, :],
                                         ALU.mult, ALU.add).then_inc(h2_total_ready, 1)

            def late_sums(t, b, earlier, base):
                sum_gathered(t, b, 0, (earlier + 1) * 16 * PER_GROUP)
                sum_gathered(t, b, 1, (earlier + 1) * 16 * PER_GROUP)
                pick_scan_rows(t, b)
                sum_gathered(t, b, 2, 16 * PER_GROUP + earlier * 16 * LATER_LAST, LATER_LAST)
                split_gathered(t, b, base)

            def tile(t, b, turn, base, first=False):
                if not first:
                    weigh_units(t - 1)
                    build_onehot(t + 2, b, (turn + 2) * 16 * BROADCASTS)
                late_sums(t + 1, 1 - b, turn + b, base)
                if first:
                    build_onehot(t + 2, b, (turn + 2) * 16 * BROADCASTS)
                build_scan_onehot(t + 2, b)
                pick_rows(t + 2, b, 0)
                pick_rows(t + 2, b, 1)
                multiply_pairs(t + 1, 1 - b, 0)
                pick_rows(t + 2, b, 2)
                multiply_pairs(t + 1, 1 - b, 1)

            sum_scanned(0)
            pick_rows(2, 0, 0)
            pick_rows(2, 0, 1)
            multiply_pairs(1, 1, 0)
            sum_scanned(1)
            pick_rows(2, 0, 2)
            multiply_pairs(1, 1, 1)
            weigh_units(0)
            sum_scanned(2)
            build_scan_onehot(2, 0)
            sum_scanned(3)
            tile(1, 1, 0, 0, first=True)
            before = steps[0]
            with dve.Fori(1, TURNS - 1) as turn:
                for b in range(2):
                    t = turn * 2 + b
                    steps[0] = before
                    tile(t, b, turn, (t - 2) * SPLIT_STEPS)
            steps[0] = before
            weigh_units(TILES - 3)
            t, b, base = TILES - 1, 1, (TILES - 4) * SPLIT_STEPS

            def chunk_gathered(c):
                dve.wait_ge(gather_in[b][c], 16 * (PER_GROUP * (TURNS - 1) + NG - 1))
                dve.tensor_reduce(gsum[:, b, 0:NG - 1, c], gathered[:, b, c * (NG - 1):(c + 1) * (NG - 1), :],
                                  AX.X, ALU.add).then_inc(gather_summed, 1)
                dve.wait_ge(gather_summed, t * GROUPS + c + 1)
                split([gparts[:, b, c, k, 0:NG] for k in range(PARTS)], gsum[:, b, :, c],
                      [grest[:, b, k, :, c] for k in range(2)], base).then_inc(gather_split, 1)

            def multiply_chunk(c, ps):
                cols = slice(c * P, (c + 1) * P)
                dve.wait_ge(right_copied, t * 2 + c + 1)
                right_of_chunk = right[:, c, :, :].rearrange("p k n -> p (k n)")
                last = (KT - 1) * P
                dve.tensor_tensor(z[:, b, 0:KT - 1, cols], ps[:, 0:last].rearrange("p (k n) -> p k n", n=P),
                                  right_of_chunk[:, 0:last].rearrange("p (k n) -> p k n", n=P), ALU.mult
                                  ).then_inc(z_ready, 1)
                dve.tensor_tensor(z[0:PAIR_ROWS_LAST, b, KT - 1, cols], ps[0:PAIR_ROWS_LAST, last:last + P],
                                  right_of_chunk[0:PAIR_ROWS_LAST, last:last + P], ALU.mult).then_inc(z_ready, 1)

            chunk_gathered(0)
            pick_scan_rows(t, b)
            multiply_chunk(0, ps_left)
            chunk_gathered(1)
            weigh_units(TILES - 2)
            multiply_chunk(1, ps_look[0])

        @bl.tensor
        def _(pe):
            def look_up(t, b, i):
                for q in (2 * i, 2 * i + 1):
                    for g in range(STRIPS):
                        s = g * PACKS + q
                        last = pe.matmul(ps_look[i % 2][g * STRIP:(g + 1) * STRIP, q % 2 * TB:(q % 2 + 1) * TB],
                                         sum_parts[:, s, :], onehot[:, b, s, :], start=True, stop=True,
                                         tile_position=(0, g * STRIP))
                last.then_inc(looked_up, 1)

            def look_up_scanned(t, b, i):
                pe.wait_ge(scan_split, 1)
                pe.wait_ge(scan_onehot_built, t - FIRST_SCANNED + 1)
                pe.wait_ge(row_picked, t * PAIRS_OF_PACKS + i + 2)
                for part in ((0, 1), (2,))[i]:
                    last = pe.matmul(ps_look[1 - i][0:SCAN_ROWS, part % 2 * TB:(part % 2 + 1) * TB],
                                     scan_parts[0:BLOCKS, part, :], scan_onehot[0:BLOCKS, b, :],
                                     start=True, stop=True)
                last.then_inc(scan_looked_up, 1)

            def transposed_sums(t, b, scanned):
                pe.wait_ge(row_picked, t * PAIRS_OF_PACKS + PAIRS_OF_PACKS)
                for q in range(PACKS):
                    pe.matmul(ps_sum, sel_rows[:, q, :], picked[:, b, q, :], start=(q == 0), stop=False)
                if scanned:
                    pe.wait_ge(scan_row_picked, t * 2)
                    for part in range(PARTS):
                        pe.matmul(ps_sum, sel_scan[:, part, :], scan_picked[0:SCAN_ROWS, b, part, :],
                                  start=False, stop=False)
                pe.wait_ge(gather_split, t + 1)
                for c in range(TILE_CHUNKS):
                    last = pe.matmul(ps_sum[:, c * P:(c + 1) * P],
                                     gparts[:, b, c, :, :].rearrange("p k f -> p (k f)"), ident,
                                     start=False, stop=(c == TILE_CHUNKS - 1))
                last.then_inc(sums_in_psum, 1)

            def pair_factors(t, b, half, banks=(ps_left, ps_right)):
                for k in range(2):
                    for side, ps in enumerate(banks):
                        last = pe.matmul(ps[:, k * TB:(k + 1) * TB], sel_pair[:, 2 * half + k, side, :],
                                         sums_t[:, b, :], start=True, stop=True)
                last.then_inc(pairs_in_psum, 1)

            def prepare_apart(t, b):
                transposed_sums(t, b, False)
                pe.wait_ge(sums_copied, t + 1)
                pair_factors(t, b, 0)
                pair_factors(t, b, 1, (ps_h2, ps_s))

            def third_layer(t, out=ps_y):
                pe.wait_ge(h2_total_ready, t + 1)
                pe.matmul(out, count_sb[:, 5:6], h2_total[:, :], start=True, stop=True).then_inc(y_in_psum, 1)

            def tile(t, b, prepare, look, first=False, scanned=True, third=True, sums_at=KT):
                first_layer(t, b, third, first, scanned, sums_at, prepare)
                second_layer(t, b, look, prepare, sums_at)

            def first_layer(t, b, third=True, first=False, scanned=True, sums_at=KT, prepare=False):
                pe.wait_ge(z_ready, t * 3 + 1)
                for n in range(KT):
                    if n == 1 and third:
                        third_layer(t - 1)
                    if n == sums_at - 1 and scanned:
                        for i in range(2):
                            look_up_scanned(t + 1, 1 - b, i)
                    if n == 1 and first:
                        pe.wait_ge(row_picked, PAIRS_OF_PACKS + 1)
                        pe.wait_ge(act_onehot_built, PACKS + ACT_PACKS)
                        look_up(1, 1, PAIRS_OF_PACKS - 1)
                    if n == 2 and not first:
                        pe.wait_ge(y_copied, t)
                    if n == sums_at and prepare:
                        transposed_sums(t + 1, 1 - b, True)
                    for k in range(KT):
                        if n == 0 and k == 2:
                            pe.wait_ge(dense_in[b], (t + 2 - b) * 8)
                            pe.wait_ge(z_ready, t * 3 + 3)
                        last = pe.matmul(ps_h1[n // 2][:, n % 2 * TB:(n % 2 + 1) * TB],
                                         W1_sb[:, k, n * P:(n + 1) * P], z[:, b, k, :],
                                         start=(k == 0), stop=(k == KT - 1))
                    if n % 2:
                        last.then_inc(h1_in_psum, 1)

            def second_layer(t, b, look, prepare, sums_at):
                if sums_at == KT and prepare:
                    transposed_sums(t + 1, 1 - b, True)
                if look:
                    pe.wait_ge(onehot_built, t + 2)
                    look_up(t + 2, b, 0)
                    look_up(t + 2, b, 1)
                for n in range(NT2):
                    if prepare:
                        if n == 0:
                            pe.wait_ge(sums_copied, t + 2)
                        else:
                            pe.wait_ge(z_ready, t * 3 + 4)
                        pair_factors(t + 1, 1 - b, n)
                    if n == 0:
                        pe.wait_ge(weights_in, 32)
                    for k in range(KT):
                        if n == 0:
                            pe.wait_ge(h1_ready, t * KT + k + 1)
                        last = pe.matmul(ps_second[n], W2_sb[:, k, n * P:(n + 1) * P], h1[:, k, :],
                                         start=(k == 0), stop=(k == KT - 1))
                    last.then_inc(h2_in_psum, 1)
                    if look and n == 0:
                        pe.wait_ge(row_picked, (t + 2) * PAIRS_OF_PACKS + 1)
                        pe.wait_ge(act_onehot_built, PACKS + (t + 2) * ACT_PACKS)
                        look_up(t + 2, b, 2)

            for i in range(PAIRS_OF_PACKS):
                pe.wait_ge(act_onehot_built, 2 * i + 2)
                pe.wait_ge(tables_split, i + 1)
                if i == PAIRS_OF_PACKS - 1:
                    pe.wait_ge(row_picked, 1)
                look_up(0, 0, i)
            pe.wait_ge(const_in, 16)
            prepare_apart(0, 0)
            pe.wait_ge(onehot_built, 1)
            look_up(1, 1, 0)
            look_up(1, 1, 1)
            pe.wait_ge(first_weights_in, 16 * KT)
            tile(0, 0, True, True, first=True, scanned=False, third=False, sums_at=KT - 1)
            tile(1, 1, True, True)
            with pe.Fori(1, TURNS - 1) as turn:
                for b in range(2):
                    tile(turn * 2 + b, b, True, True)
            t, b = TILES - 1, 1
            halves = [slice(c * P, (c + 1) * P) for c in range(TILE_CHUNKS)]
            factors = [(ps_left, ps_right), ps_look]
            second = [(ps_h2, ps_s), ps_look]

            def chunk_sums(c):
                for q in range(PACKS):
                    pe.matmul(ps_sum[:, halves[c]], sel_rows[:, q, :], picked[:, b, q, halves[c]],
                              start=(q == 0), stop=False)
                for part in range(PARTS):
                    pe.matmul(ps_sum[:, halves[c]], sel_scan[:, part, :],
                              scan_picked[0:SCAN_ROWS, b, part, halves[c]], start=False, stop=False)
                pe.wait_ge(gather_split, t + c + 1)
                pe.matmul(ps_sum[:, halves[c]], gparts[:, b, c, :, :].rearrange("p k f -> p (k f)"), ident,
                          start=False, stop=True).then_inc(sums_in_psum, 1)

            def chunk_factors(c):
                pe.wait_ge(sums_copied, t + c + 1)
                for k in range(KT):
                    for side in range(2):
                        last = pe.matmul(factors[c][side][:, k * P:(k + 1) * P], sel_pair[:, k, side, :],
                                         sums_t[:, b, halves[c]], start=True, stop=True)
                last.then_inc(pairs_in_psum, 1)

            def chunk_first_layer(c, n):
                for k in range(KT):
                    last = pe.matmul(ps_h1[n // 2][:, n % 2 * P:(n % 2 + 1) * P], W1_sb[:, k, n * P:(n + 1) * P],
                                     z[:, b, k, halves[c]], start=(k == 0), stop=(k == KT - 1))
                if n % 2:
                    last.then_inc(h1_in_psum, 1)

            def chunk_second_layer(c):
                for n in range(NT2):
                    for k in range(KT):
                        if n == 0:
                            pe.wait_ge(h1_ready, (t + c) * KT + k + 1)
                        last = pe.matmul(second[c][n][:, 0:P], W2_sb[:, k, n * P:(n + 1) * P], h1[:, k, halves[c]],
                                         start=(k == 0), stop=(k == KT - 1))
                    last.then_inc(h2_in_psum, 1)

            def chunk_third_layer(c):
                for k in range(NT2):
                    pe.wait_ge(h2_ready, (t + c) * NT2 + k + 1)
                    last = pe.matmul(ps_y_chunk[c], W3_sb[:, k:k + 1], h2[:, k, halves[c]],
                                     start=(k == 0), stop=(k == NT2 - 1))
                last.then_inc(y_in_psum, 1)

            first_layer(TILES - 2, 0)
            pe.wait_ge(row_picked, TILES * PAIRS_OF_PACKS)
            pe.wait_ge(scan_row_picked, t * 2)
            chunk_sums(0)
            for n in range(NT2):
                if n == 1:
                    chunk_factors(0)
                for k in range(KT):
                    if n == 0:
                        pe.wait_ge(h1_ready, (t - 1) * KT + k + 1)
                    last = pe.matmul(ps_second_late[n], W2_sb[:, k, n * P:(n + 1) * P], h1[:, k, :],
                                     start=(k == 0), stop=(k == KT - 1))
                last.then_inc(h2_in_psum, 1)
            pe.wait_ge(dense_in[b], TILES * 8)
            pe.wait_ge(z_ready, t * 3 + 2)
            for n in range(KT):
                if n == KT - 1:
                    chunk_sums(1)
                chunk_first_layer(0, n)
            third_layer(TILES - 2, ps_y_late)
            chunk_factors(1)
            chunk_second_layer(0)
            pe.wait_ge(z_ready, t * 3 + 4)
            for n in range(KT):
                chunk_first_layer(1, n)
            chunk_third_layer(0)
            chunk_second_layer(1)
            chunk_third_layer(1)


def kernel(**inputs):
    import concourse.bacc as _bacc
    from concourse.bass_utils import run_bass_kernel_spmd as _run

    nc = _bacc.Bacc("TRN2", target_bir_lowering=False, num_devices=1)
    a = {k: np.ascontiguousarray(v) for k, v in inputs.items()}
    ids = a["ids"].reshape(P, CHUNKS, FIELDS)
    by_slot = ids[:, :, [SMALL[0] if f is None else f for f in TABLE]]
    by_slot = by_slot.reshape(P, TILES, TILE_CHUNKS, 2, SLOTS // 2).transpose(3, 1, 4, 2, 0)
    ones, counters = constants()
    packed = np.zeros((PACKS, P, sum(ROWS) * DIM), np.float32)
    for s, f in enumerate(TABLE):
        g, q = divmod(s, PACKS)
        if f is not None:
            packed[q, :BLOCKS, sum(ROWS[:g]) * DIM:sum(ROWS[:g + 1]) * DIM] = a[f"tbl_{f}"].reshape(BLOCKS, -1)
    arrays = {
        "ids_rows": ids[:, :, GATHERED],
        "small_tables": packed,
        "ids_slots": by_slot.reshape(P, NUMBERS),
        "ids_scan": ids[:, :, SCANNED].T.reshape(P, CHUNKS),
        "dense_t": a["dense_ctx"].reshape(P, TILES, TILE_CHUNKS, DENSE).transpose(1, 3, 2, 0).reshape(TILES, DENSE, TB),
        "W1": a["W_top1"], "b1": a["b_top1"].reshape(KT, P).T,
        "W2": a["W_top2"], "b2": a["b_top2"].reshape(NT2, P).T,
        "W3": a["W_top3"].reshape(NT2, P).T, "ones": ones, "counters": counters,
    }
    for f in GATHERED:
        arrays[f"tbl_{f}"] = a[f"tbl_{f}"]
    arrays = {k: np.ascontiguousarray(v) for k, v in arrays.items()}
    ap = {k: nc.dram_tensor(f"in_{k}", v.shape, mybir.dt.from_np(v.dtype), kind="ExternalInput").ap()
          for k, v in arrays.items()}
    out = nc.dram_tensor("out_y", (1, BATCH), mybir.dt.float32, kind="ExternalOutput").ap()
    dlrm_tower(nc, ap["ids_rows"], ap["ids_slots"], ap["ids_scan"], ap["dense_t"], ap["small_tables"],
               {f: ap[f"tbl_{f}"] for f in GATHERED},
               ap["W1"], ap["b1"], ap["W2"], ap["b2"], ap["W3"], ap["ones"], ap["counters"], out)
    r = _run(nc, [{f"in_{k}": v for k, v in arrays.items()}], core_ids=[0])
    return r.results[0]["out_y"].reshape(CHUNKS, P).T.reshape(BATCH, 1)
```
